# Optimizing a Trainium2 kernel written in Bass

```python
import numpy as np
import jax
import jax.numpy as jnp

def _softmax(x, axis=-1):
    return jax.nn.softmax(x, axis=axis)

def _gelu(x):
    return jax.nn.gelu(x, approximate=True)

def _silu(x):
    return jax.nn.silu(x)

def _sigmoid(x):
    return jax.nn.sigmoid(x)

def _layernorm(x, axis=-1, eps=1e-05):
    m = jnp.mean(x, axis=axis, keepdims=True)
    v = jnp.var(x, axis=axis, keepdims=True)
    return (x - m) / jnp.sqrt(v + eps)

def _scatter_add(tgt, idx, src, axis=0):
    return tgt.at[idx].add(src)

def _segment_sum(src, seg, n):
    return jax.ops.segment_sum(src, seg, n)
kernel_name = 'mk_conv_preact_d1_conv_nhwc512_r2_c3d0ce'

def setup_inputs(seed: int=0):
    np.random.seed(seed)
    _w = jnp.asarray

    def _rec_inputs():
        import jax
        import jax.numpy as jnp
        _gk = jax.random.key(seed)
        x = -0.0003957 + 1 * jax.random.normal(jax.random.fold_in(_gk, 1), (8, 56, 56, 256), jnp.float32)
        return x
    x = _rec_inputs()

    def _L0_conv_setup():
        import jax, jax.numpy as jnp
        import numpy as np
        DIM = 256
        HEADS = 8
        HEAD_DIM = DIM // HEADS
        N_WIN = 7
        TOPK = 4
        SCALE = DIM ** (-0.5)

        def _grid2seq(t, rs):
            B, C, H, W = t.shape
            rh, rw = (H // rs[0], W // rs[1])
            t = t.reshape(B, HEADS, HEAD_DIM, rh, rs[0], rw, rs[1])
            t = t.transpose(0, 1, 3, 5, 4, 6, 2)
            return (t.reshape(B, HEADS, rh * rw, rs[0] * rs[1], HEAD_DIM), rh, rw)

        def _seq2grid(t, rh, rw, rs):
            B, m, nreg, _, d = t.shape
            t = t.reshape(B, m, rh, rw, rs[0], rs[1], d)
            t = t.transpose(0, 1, 6, 2, 4, 3, 5)
            return t.reshape(B, m * d, rh * rs[0], rw * rs[1])
        key = jax.random.key(seed)
        ks = jax.random.split(key, 7)
        B, H, W = (8, 56, 56)
        x = jax.random.normal(ks[0], (B, H, W, DIM), dtype=jnp.float32)
        qkv_w = jax.random.normal(ks[1], (3 * DIM, DIM), dtype=jnp.float32) * DIM ** (-0.5)
        qkv_b = jnp.zeros((3 * DIM,), dtype=jnp.float32)
        lepe_w = jax.random.normal(ks[2], (DIM, 1, 3, 3), dtype=jnp.float32) * 0.1
        lepe_b = jnp.zeros((DIM,), dtype=jnp.float32)
        out_w = jax.random.normal(ks[3], (DIM, DIM), dtype=jnp.float32) * DIM ** (-0.5)
        out_b = jnp.zeros((DIM,), dtype=jnp.float32)
        return {'x': x, 'qkv_w': qkv_w, 'qkv_b': qkv_b, 'lepe_w': lepe_w, 'lepe_b': lepe_b, 'out_w': out_w, 'out_b': out_b}
    _L0_conv_all = _L0_conv_setup()
    _L0_conv_in = {k: v for k, v in _L0_conv_all.items() if k in ('qkv_w', 'qkv_b', 'lepe_w', 'lepe_b', 'out_w', 'out_b')}
    del _L0_conv_all
    return {'x': x, 'L0_conv_qkv_w': _L0_conv_in['qkv_w'], 'L0_conv_qkv_b': _L0_conv_in['qkv_b'], 'L0_conv_lepe_w': _L0_conv_in['lepe_w'], 'L0_conv_lepe_b': _L0_conv_in['lepe_b'], 'L0_conv_out_w': _L0_conv_in['out_w'], 'L0_conv_out_b': _L0_conv_in['out_b']}

def reference(x, L0_conv_qkv_w, L0_conv_qkv_b, L0_conv_lepe_w, L0_conv_lepe_b, L0_conv_out_w, L0_conv_out_b):
    import jax
    import jax.numpy as jnp

    def _L0_conv_ref(x, qkv_w, qkv_b, lepe_w, lepe_b, out_w, out_b):
        import jax, jax.numpy as jnp
        import numpy as np
        DIM = 256
        HEADS = 8
        HEAD_DIM = DIM // HEADS
        N_WIN = 7
        TOPK = 4
        SCALE = DIM ** (-0.5)

        def _grid2seq(t, rs):
            B, C, H, W = t.shape
            rh, rw = (H // rs[0], W // rs[1])
            t = t.reshape(B, HEADS, HEAD_DIM, rh, rs[0], rw, rs[1])
            t = t.transpose(0, 1, 3, 5, 4, 6, 2)
            return (t.reshape(B, HEADS, rh * rw, rs[0] * rs[1], HEAD_DIM), rh, rw)

        def _seq2grid(t, rh, rw, rs):
            B, m, nreg, _, d = t.shape
            t = t.reshape(B, m, rh, rw, rs[0], rs[1], d)
            t = t.transpose(0, 1, 6, 2, 4, 3, 5)
            return t.reshape(B, m * d, rh * rs[0], rw * rs[1])
        xc = x.transpose(0, 3, 1, 2)
        N, C, H, W = xc.shape
        rs = (H // N_WIN, W // N_WIN)
        qkv = jnp.einsum('nchw,oc->nohw', xc, qkv_w) + qkv_b[None, :, None, None]
        q, k, v = jnp.split(qkv, 3, axis=1)

        def pool(t):
            t = t.reshape(N, C, N_WIN, rs[0], N_WIN, rs[1])
            return t.mean(axis=(3, 5))
        q_r = jax.lax.stop_gradient(pool(q)).transpose(0, 2, 3, 1).reshape(N, N_WIN * N_WIN, C)
        k_r = jax.lax.stop_gradient(pool(k)).reshape(N, C, N_WIN * N_WIN)
        a_r = q_r @ k_r
        _, idx_r = jax.lax.top_k(a_r, TOPK)
        idx_r = jnp.broadcast_to(idx_r[:, None], (N, HEADS, N_WIN * N_WIN, TOPK))
        qs, rh, rw = _grid2seq(q, rs)
        ks_, _, _ = _grid2seq(k, rs)
        vs, _, _ = _grid2seq(v, rs)
        bsz, nh, kv_nreg, kv_rsz, hd = ks_.shape
        q_nreg = qs.shape[2]
        idx = idx_r[:, :, :, :, None, None]
        key_g = jnp.take_along_axis(ks_[:, :, None], idx, axis=3)
        val_g = jnp.take_along_axis(vs[:, :, None], idx, axis=3)
        key_g = key_g.reshape(bsz, nh, q_nreg, TOPK * kv_rsz, hd)
        val_g = val_g.reshape(bsz, nh, q_nreg, TOPK * kv_rsz, hd)
        attn = jnp.einsum('bhnqd,bhnkd->bhnqk', qs * SCALE, key_g)
        attn = jax.nn.softmax(attn, axis=-1)
        out = jnp.einsum('bhnqk,bhnkd->bhnqd', attn, val_g)
        out = _seq2grid(out, rh, rw, rs)
        lepe = jax.lax.conv_general_dilated(v, lepe_w, window_strides=(1, 1), padding='SAME', feature_group_count=DIM, dimension_numbers=('NCHW', 'OIHW', 'NCHW'))
        lepe = lepe + lepe_b[None, :, None, None]
        out = out + lepe
        out = jnp.einsum('nchw,oc->nohw', out, out_w) + out_b[None, :, None, None]
        return out.transpose(0, 2, 3, 1)

    def _gn(v, G=32, eps=1e-05):
        B_, H_, W_, C_ = v.shape
        g = v.reshape(B_, H_, W_, G, C_ // G)
        m = jnp.mean(g, axis=(1, 2, 4), keepdims=True)
        s = jnp.var(g, axis=(1, 2, 4), keepdims=True)
        return ((g - m) / jnp.sqrt(s + eps)).reshape(v.shape)

    def _ln_c(v, eps=1e-06):
        m = jnp.mean(v, axis=-1, keepdims=True)
        s = jnp.var(v, axis=-1, keepdims=True)
        return (v - m) / jnp.sqrt(s + eps)

    def _ln_t(v, eps=1e-05):
        m = jnp.mean(v, axis=-1, keepdims=True)
        s = jnp.var(v, axis=-1, keepdims=True)
        return (v - m) / jnp.sqrt(s + eps)

    def _to_tokens(v):
        B_, H_, W_, C_ = v.shape
        return v.reshape(B_, H_ * W_, C_)

    def _from_tokens(t, like):
        return t.reshape(like.shape)
    x = x + _L0_conv_ref(_gn(x), L0_conv_qkv_w, L0_conv_qkv_b, L0_conv_lepe_w, L0_conv_lepe_b, L0_conv_out_w, L0_conv_out_b)
    return x

_drawn_inputs = setup_inputs


def setup_inputs(seed=0):
    import zlib

    import numpy as np

    out = dict(_drawn_inputs(seed))
    spreads = {'L0_conv_qkv_b': (0.0, 0.1), 'L0_conv_lepe_b': (0.0, 0.1), 'L0_conv_out_b': (0.0, 0.1)}
    factors = {}
    for name, (base, spread) in spreads.items():
        noise = np.random.default_rng([zlib.crc32(name.encode()), seed]).standard_normal(out[name].shape)
        drawn = base * np.exp(spread * noise) if base else spread * noise
        out[name] = jnp.asarray(drawn.astype(out[name].dtype))
    for name, factor in factors.items():
        out[name] = (out[name] * factor).astype(out[name].dtype)
    return out
```

```python
from contextlib import ExitStack

import concourse.bass as bass
from concourse import mybir

F32 = mybir.dt.float32
U32 = mybir.dt.uint32
ALU = mybir.AluOpType
ACT = mybir.ActivationFunctionType
AX = mybir.AxisListType

P = 128
NB, H, W, C = 8, 56, 56, 256
HEADS, HD = 8, 32
NWIN, TOPK = 7, 4
RS = H // NWIN
RT = RS * RS
NREG = NWIN * NWIN
ROW = RS * W
TOK = H * W
KC = C // P
HG = P // HD
PAIRS = HEADS // 2
KEYS = TOPK * RT
CH = KEYS // P
TT = 2 * W
NT = ROW // TT
PADW = W + 2
GROUP = C // 32
EPS = 1e-5
SCALE = C ** -0.5
TAPS = 9


def attention_kernel(nc, x, w_qkv, w_out, b_qkv, b_out, w_tap, b_tap, ident_d, group_d, out):
    x_rows = x.rearrange("g (j p) c -> g p j c", p=TT)
    out_rows = out.rearrange("g (j p) c -> g p j c", p=TT)
    x_img = x.rearrange("(b r) (j p) c -> b p (r j) c", b=NB, p=TT)

    with ExitStack() as ctx:
        def sb(name, shape, dt=F32):
            return ctx.enter_context(nc.sbuf_tensor(name, shape, dt))

        def sem(name):
            return ctx.enter_context(nc.semaphore(name))

        wqkv = sb("wqkv", [P, KC, 3 * C])
        wout = sb("wout", [P, KC, C])
        bqkv = sb("bqkv", [P, 3 * KC])
        bq_scaled = sb("bq_scaled", [P, KC])
        bout = sb("bout", [TT, C])
        taps = sb("taps", [P, KC, TAPS])
        btap = sb("btap", [P, KC])
        ident = sb("ident", [P, P])
        group = sb("group", [P, P])
        x_tok = sb("x_tok", [P, NWIN * NT * C])
        x_in = x_tok[0:TT, :].rearrange("p (t c) -> p t c", c=C)
        v_pad = x_tok[:, 0:KC * PADW * PADW].rearrange("p (k r c) -> p k r c", k=KC, r=PADW)
        xn = sb("xn", [P, KC, TOK])
        k_all = sb("k_all", [P, KC, TOK])
        v_tok = sb("v_tok", [RT, NREG, C])
        lepe = sb("lepe", [P, KC, TOK])
        q_blocks = sb("q_blocks", [P, KC, NWIN, HG, RT])
        o_row = sb("o_row", [P, KC, ROW])
        resid = sb("resid", [TT, NT, C])
        o_stage = sb("o_stage", [TT, NT, C])
        probs = sb("probs", [P, PAIRS, KEYS])
        v_row = probs[:, :, :].rearrange("p a b -> p (a b)")[:, 0:KC * ROW].rearrange("p (k t) -> p k t", k=KC)
        probs_t = sb("probs_t", [P, CH, HEADS * RT])
        k_sel = sb("k_sel", [P, 2, KC, KEYS])
        v_sel = sb("v_sel", [P, 2, CH, C])
        neg_max = sb("neg_max", [P, PAIRS])
        denom = sb("denom", [P, PAIRS])
        rdenom = sb("rdenom", [P, PAIRS])
        stats = sb("stats", [P, KC, NWIN, 6])
        mv = sb("mv", [P, KC, 2])
        dev = sb("dev", [P, KC])
        var2 = sb("var2", [P, KC])
        rstd = sb("rstd", [P, KC])
        neg_half = sb("neg_half", [P, KC])
        shift = sb("shift", [P, KC])
        x_sum = sb("x_sum", [P, KC, NREG])
        qk_mean = sb("qk_mean", [P, 2 * KC, NREG])
        affinity = sb("affinity", [NREG, NREG])
        top = sb("top", [NREG, 8])
        top_idx = sb("top_idx", [NREG, 8], U32)
        idx_row = sb("idx_row", [1, NREG * TOPK], U32)

        bank = [ctx.enter_context(nc.psum_tensor(f"bank{i}", [P, 512], F32)) for i in range(8)]

        weights_in, x_in_done, idx_in = sem("weights_in"), sem("x_in_done"), sem("idx_in")
        v_sel_in = [sem("v_sel_in0"), sem("v_sel_in1")]
        resid_in, out_stored = sem("resid_in"), sem("out_stored")
        waits_passed = sem("waits_passed")
        dve_self = sem("dve_self")
        setup_done, zeros_done = sem("setup_done"), sem("zeros_done")
        x_turned, x_evac, stats_done, mean_done, mean_taken, var_done = map(
            sem, ("x_turned", "x_evac", "stats_done", "mean_done", "mean_taken", "var_done"))
        var_ready, scale_ready, row_normed, region_sums = map(sem, ("var_ready", "scale_ready", "row_normed", "region_sums"))
        var_eps, rstd_ready = sem("var_eps"), sem("rstd_ready")
        v_proj, k_proj, v_evac, k_evac, v_turned, v_tok_evac, pad_clear, pad_evac = map(
            sem, ("v_proj", "k_proj", "v_evac", "k_evac", "v_turned", "v_tok_evac", "pad_clear", "pad_evac"))
        means_proj, means_evac, affinity_done, top_done, lepe_done = map(
            sem, ("means_proj", "means_evac", "affinity_done", "top_done", "lepe_done"))
        q_proj, q_evac_act, q_evac_dve = sem("q_proj"), sem("q_evac_act"), sem("q_evac_dve")
        k_sel_done, scores_done, max_done, exp_done, probs_done = map(
            sem, ("k_sel_done", "scores_done", "max_done", "exp_done", "probs_done"))
        probs_turned, probs_t_evac, attn_done, o_row_done, out_proj, out_evac, resid_ready = map(
            sem, ("probs_turned", "probs_t_evac", "attn_done", "o_row_done", "out_proj", "out_evac", "resid_ready"))

        def by_region(flat):
            return flat.rearrange("p (g r c) -> p r g c", g=NWIN, r=RS)

        def by_image(flat):
            return flat.rearrange("p (r g c) -> p r g c", r=RS, g=NWIN)

        def q_block(s, k, h):
            return q_blocks[s, k, :, h, :].rearrange("p g (r c) -> p r g c", r=RS)

        def slot_uses(g, rc):
            return g * (4 if rc % 2 == 0 else 3) + rc // 2 + 1

        N_WEIGHTS = 8

        def wait_alone(eng, semaphore, value):
            eng.wait_ge(semaphore, value)
            eng.sem_inc(waits_passed, 1)

        block = ctx.enter_context(nc.Block())

        @block.sync
        def _(sp):
            sp.dma_start(x_in, x_img[0]).then_inc(x_in_done, 16)
            sp.dma_start(ident[:], ident_d).then_inc(weights_in, 16)
            sp.dma_start(group[:], group_d).then_inc(weights_in, 16)
            sp.dma_start(wqkv[:], w_qkv.rearrange("(k p) o -> p k o", p=P)).then_inc(weights_in, 16)
            sp.dma_start(bqkv[:], b_qkv).then_inc(weights_in, 16)
            sp.dma_start(taps[:], w_tap).then_inc(weights_in, 16)
            sp.dma_start(btap[:], b_tap).then_inc(weights_in, 16)
            sp.dma_start(wout[:], w_out.rearrange("(k p) o -> p k o", p=P)).then_inc(weights_in, 16)
            sp.dma_start(bout[:], b_out).then_inc(weights_in, 16)

            def store_row(g):
                sp.wait_ge(out_evac, 2 * g + 2)
                sp.dma_start(out_rows[g], o_stage[:]).then_inc(out_stored, 16)

            def regions(b, rr):
                g = b * NWIN + rr
                for rc in range(NWIN):
                    r = g * NWIN + rc
                    wait_alone(sp, attn_done, r - 1 if rc else r)
                    for j in range(TOPK):
                        reg = sp.value_load(idx_row[0:1, bass.ds((rr * NWIN + rc) * TOPK + j, 1)],
                                            min_val=0, max_val=NREG - 1)
                        half = RT * (j % 2)
                        sp.dma_start(v_sel[half:half + RT, rc % 2, j // 2, :],
                                     v_tok[:, bass.ds(reg, 1), :]).then_inc(v_sel_in[rc % 2], 16)
                    if rc == 2:
                        sp.wait_ge(out_evac, 2 * g)
                        sp.dma_start(resid[:], x_rows[g]).then_inc(resid_in, 16)

            def image(b, last):
                sp.wait_ge(top_done, b + 1)
                sp.dma_start(idx_row[:], top_idx[:, 0:TOPK]).then_inc(idx_in, 16)
                wait_alone(sp, idx_in, 16 * (b + 1))
                wait_alone(sp, v_tok_evac, 4 * NWIN * (b + 1))
                regions(b, 0)
                if not last:
                    sp.wait_ge(lepe_done, NWIN * (b + 1))
                    sp.dma_start(x_in, x_img[b + 1]).then_inc(x_in_done, 16)
                with sp.Fori(1, NWIN) as rr:
                    store_row(b * NWIN + rr - 1)
                    regions(b, rr)
                store_row(b * NWIN + NWIN - 1)

            with sp.Fori(0, NB - 1) as b:
                image(b, False)
            image(NB - 1, True)
            sp.wait_ge(out_stored, 16 * NB * NWIN)

        @block.gpsimd
        def _(pool):
            pool.memset(neg_half[:], -0.5).then_inc(zeros_done, 1)
            pool.memset(q_blocks[:, :, :, :, :], 0.0).then_inc(zeros_done, 1)

            def add_bias(g):
                pool.wait_ge(resid_in, 16 * (g + 1))
                pool.tensor_tensor(resid[:], resid[:], bout[:, :].unsqueeze(1).to_broadcast([TT, NT, C]),
                                   ALU.add).then_inc(resid_ready, 1)

            def regions(b, rr):
                g = b * NWIN + rr
                for rc in range(NWIN):
                    r = g * NWIN + rc
                    pool.wait_ge(scores_done, PAIRS * (r - 1) if rc else PAIRS * r)
                    for j in range(TOPK):
                        reg = pool.value_load(idx_row[0:1, bass.ds((rr * NWIN + rc) * TOPK + j, 1)],
                                              min_val=0, max_val=NREG - 1)
                        last = pool.tensor_copy(k_sel[:, rc % 2, :, RT * j:RT * (j + 1)],
                                                k_all[:, :, bass.ds(reg * RT, RT)])
                    last.then_inc(k_sel_done, 1)
                    if rc == 4:
                        add_bias(g)

            pool.wait_ge(weights_in, 16 * N_WEIGHTS)
            with pool.Fori(0, NB) as b:
                pool.wait_ge(zeros_done, 2)
                pool.wait_ge(var_eps, b + 1)
                pool.tensor_tensor(rstd[:], var2[:], neg_half[:], ALU.pow).then_inc(rstd_ready, 1)
                wait_alone(pool, x_turned, KC * NWIN * (b + 1))
                pool.memset(v_pad[:, :, 0:PADW:PADW - 1, :], 0.0).then_inc(pad_clear, 1)
                pool.memset(v_pad[:, :, 1:PADW - 1, 0:PADW:PADW - 1], 0.0).then_inc(pad_clear, 1)
                with pool.Fori(0, NWIN) as rr:
                    pool.wait_ge(v_evac, KC * (b * NWIN + rr + 1))
                    for k in range(KC):
                        last = pool.tensor_copy(
                            v_pad[:, k, bass.ds(rr * RS + 1, RS), 1:1 + W].rearrange("p r (g c) -> p r g c", g=NWIN),
                            by_region(v_row[:, k, :]))
                    last.then_inc(pad_evac, 1)
                pool.wait_ge(idx_in, 16 * (b + 1))
                wait_alone(pool, k_evac, KC * NWIN * (b + 1))
                with pool.Fori(0, NWIN) as rr:
                    regions(b, rr)

        @block.scalar
        def _(act):
            act.wait_ge(weights_in, 16 * N_WEIGHTS)
            act.wait_ge(setup_done, 1)

            def q_blocks_evac(g):
                act.wait_ge(q_proj, 2 * g + 1)
                for h in range(HG):
                    s = slice(HD * h, HD * (h + 1))
                    last = act.activation(q_block(s, 0, h), by_image(bank[0][s, 0:ROW]), ACT.Identity,
                                          bias=bq_scaled[s, 0:1], scale=SCALE)
                last.then_inc(q_evac_act, 1)

            def probs_t_out(r):
                for c in range(CH):
                    act.wait_ge(probs_turned, CH * r + c + 1)
                    if c == 0:
                        act.wait_ge(attn_done, r)
                    act.copy(probs_t[:, c, :], bank[4 + c][:, :]).then_inc(probs_t_evac, 1)

            def exps(r):
                for p in range(PAIRS):
                    act.wait_ge(max_done, PAIRS * r + p + 1)
                    if p == 0:
                        act.wait_ge(probs_turned, CH * r)
                    act.activation(probs[:, p, :], bank[p][:, 0:KEYS], ACT.Exp, bias=neg_max[:, p:p + 1],
                                   accum_out=denom[:, p:p + 1]).then_inc(exp_done, 1)

            def regions(b, rr):
                g = b * NWIN + rr
                q_blocks_evac(g)
                for rc in range(NWIN):
                    r = g * NWIN + rc
                    exps(r)
                    probs_t_out(r)

            with act.Fori(0, NB) as b:
                for t in range(NWIN):
                    for k in range(KC):
                        n = KC * t + k
                        act.wait_ge(x_turned, KC * NWIN * b + n + 1)
                        act.copy(xn[:, k, ROW * t:ROW * (t + 1)], bank[n % 4][:, 0:ROW]).then_inc(x_evac, 1)
                act.wait_ge(scale_ready, b + 1)
                with act.Fori(0, NWIN) as rr:
                    g = b * NWIN + rr
                    for k in range(KC):
                        act.activation(xn[:, k, bass.ds(rr * ROW, ROW)], xn[:, k, bass.ds(rr * ROW, ROW)], ACT.Identity,
                                       bias=shift[:, k:k + 1], scale=rstd[:, k:k + 1]).then_inc(row_normed, 1)
                    act.wait_ge(v_turned, 4 * g)
                    act.wait_ge(pad_evac, g)
                    for k in range(KC):
                        act.wait_ge(v_proj, KC * g + k + 1)
                        act.activation(by_region(v_row[:, k, :]), by_image(bank[2 + k][:, 0:ROW]), ACT.Identity,
                                       bias=bqkv[:, 2 * KC + k:2 * KC + k + 1]).then_inc(v_evac, 1)
                    for k in range(KC):
                        act.wait_ge(k_proj, KC * g + k + 1)
                        act.activation(by_region(k_all[:, k, bass.ds(rr * ROW, ROW)]), by_image(bank[k][:, 0:ROW]),
                                       ACT.Identity, bias=bqkv[:, KC + k:KC + k + 1]).then_inc(k_evac, 1)
                    for m in range(4):
                        act.wait_ge(v_turned, 4 * g + m + 1)
                        n = min(2, NWIN - 2 * m)
                        act.copy(v_tok[:, bass.ds(rr * NWIN + 2 * m, n), :],
                                 bank[4 + m][0:RT, 0:n * C].rearrange("p (n c) -> p n c", n=n)).then_inc(v_tok_evac, 1)
                act.wait_ge(means_proj, b + 1)
                for m in range(2 * KC):
                    act.activation(qk_mean[:, m, :], bank[0][:, NREG * m:NREG * (m + 1)], ACT.Identity,
                                   bias=bqkv[:, m:m + 1], scale=1.0 / RT).then_inc(means_evac, 1)
                with act.Fori(0, NWIN) as rr:
                    regions(b, rr)

        @block.vector
        def _(dve):
            own = [0]

            def settle(ins, base):
                own[0] += 1
                ins.then_inc(dve_self, 1)
                wait_alone(dve, dve_self, base + own[0])

            dve.wait_ge(weights_in, 16 * N_WEIGHTS)
            dve.tensor_scalar(bq_scaled[:], bqkv[:, 0:KC], SCALE, None, ALU.mult).then_inc(setup_done, 1)

            PER_REGION = PAIRS
            SELF_A2 = 2
            SELF_TOP = 2
            LEPE_ROW = KC * (TAPS - 1)
            PER_IMAGE = SELF_A2 + SELF_TOP + NWIN * LEPE_ROW + NREG * PER_REGION

            def lepe_row(base, rr):
                o = [lepe[:, k, bass.ds(rr * ROW, ROW)].rearrange("p (r c) -> p r c", c=W) for k in range(KC)]
                for t in range(TAPS):
                    for k in range(KC):
                        src = v_pad[:, k, bass.ds(rr * RS + t // 3, RS), t % 3:t % 3 + W]
                        if t == 0:
                            ins = dve.tensor_scalar(o[k], src, taps[:, k, 0:1], btap[:, k:k + 1], ALU.mult, ALU.add)
                        else:
                            dve.wait_ge(dve_self, base + KC * (t - 1) + k + 1)
                            ins = dve.scalar_tensor_tensor(o[k], src, taps[:, k, t:t + 1], o[k], ALU.mult, ALU.add)
                        if t < TAPS - 1:
                            ins.then_inc(dve_self, 1)
                        elif k == KC - 1:
                            ins.then_inc(lepe_done, 1)

            def sums_row(b, rr):
                dve.wait_ge(row_normed, KC * (b * NWIN + rr + 1))
                for k in range(KC):
                    ins = dve.tensor_reduce(
                        x_sum[:, k, bass.ds(rr * NWIN, NWIN)],
                        xn[:, k, bass.ds(rr * ROW, ROW)].rearrange("p (r g c) -> p g r c", r=RS, g=NWIN), AX.XY, ALU.add)
                ins.then_inc(region_sums, 1)

            def q_blocks_evac(g):
                dve.wait_ge(q_proj, 2 * g + 2)
                for h in range(HG):
                    s = slice(HD * h, HD * (h + 1))
                    last = dve.tensor_scalar(q_block(s, 1, h), by_image(bank[1][s, 0:ROW]), SCALE,
                                             bq_scaled[s, 1:2], ALU.mult, ALU.add)
                last.then_inc(q_evac_dve, 1)

            def out_row(g):
                dve.wait_ge(resid_ready, g + 1)
                dve.wait_ge(out_stored, 16 * g)
                for m in range(2):
                    dve.wait_ge(out_proj, 2 * g + m + 1)
                    dve.tensor_tensor(o_stage[:, 2 * m:2 * m + 2, :],
                                      bank[2 + m][0:TT, :].rearrange("p (j c) -> p j c", j=2),
                                      resid[:, 2 * m:2 * m + 2, :], ALU.add).then_inc(out_evac, 1)

            def maximum(r, p):
                dve.wait_ge(scores_done, PAIRS * r + p + 1)
                dve.tensor_reduce(neg_max[:, p:p + 1], bank[p][:, 0:KEYS], AX.X, ALU.max,
                                  negate=True).then_inc(max_done, 1)

            def divide(r, p, base):
                dve.wait_ge(exp_done, PAIRS * r + p + 1)
                dve.reciprocal(rdenom[:, p:p + 1], denom[:, p:p + 1]).then_inc(dve_self, 1)
                dve.wait_ge(dve_self, base + p + 1)
                dve.tensor_scalar(probs[:, p, :], probs[:, p, :], rdenom[:, p:p + 1], None,
                                  ALU.mult).then_inc(probs_done, 1)

            def take_region(r, b, rr, rc):
                dve.wait_ge(attn_done, r + 1)
                cols = slice(RS * rc, RS * (rc + 1))
                dve.tensor_tensor(o_row[:, :, :].rearrange("p k (r c) -> p k r c", c=W)[:, :, :, cols],
                                  bank[6][:, 0:KC * RT].rearrange("p (k r c) -> p k r c", k=KC, r=RS),
                                  lepe[:, :, bass.ds(rr * ROW, ROW)].rearrange("p k (r c) -> p k r c", c=W)[:, :, :, cols],
                                  ALU.add).then_inc(o_row_done, 1)

            def regions(b, rr, first):
                g = b * NWIN + rr
                q_blocks_evac(g)
                if not first:
                    out_row(g - 1)
                for rc in range(NWIN):
                    r = g * NWIN + rc
                    base = b * PER_IMAGE + SELF_A2 + SELF_TOP + NWIN * LEPE_ROW + (rr * NWIN + rc) * PER_REGION
                    for p in range(3):
                        maximum(r, p)
                    divide(r, 0, base)
                    maximum(r, 3)
                    for p in range(1, PAIRS):
                        divide(r, p, base)
                    if rc > 0:
                        take_region(r - 1, b, rr, rc - 1)
                take_region(g * NWIN + NWIN - 1, b, rr, NWIN - 1)

            with dve.Fori(0, NB) as b:
                for t in range(NWIN):
                    for k in range(KC):
                        dve.wait_ge(x_evac, KC * NWIN * b + KC * t + k + 1)
                        last = dve.bn_stats(stats[:, k, t, :], xn[:, k, ROW * t:ROW * (t + 1)])
                last.then_inc(stats_done, 1)
                wait_alone(dve, stats_done, b + 1)
                own[0] = 0
                base = b * PER_IMAGE
                for k in range(KC):
                    last = dve.bn_aggr(mv[:, k, :], stats[:, k, :, :])
                last.then_inc(mean_done, 1)
                dve.wait_ge(mean_taken, b + 1)
                settle(dve.tensor_tensor(dev[:], mv[:, :, 0], bank[4][:, 0:KC], ALU.subtract), base)
                settle(dve.tensor_tensor(dev[:], dev[:], dev[:], ALU.mult), base)
                dve.tensor_tensor(var2[:], dev[:], mv[:, :, 1], ALU.add).then_inc(var_done, 1)
                dve.wait_ge(var_ready, b + 1)
                dve.tensor_scalar(var2[:], bank[5][:, 0:KC], EPS, None, ALU.add).then_inc(var_eps, 1)
                dve.wait_ge(rstd_ready, b + 1)
                dve.scalar_tensor_tensor(shift[:], bank[4][:, 0:KC], -1.0, rstd[:], ALU.mult,
                                         ALU.mult).then_inc(scale_ready, 1)
                sums_row(b, 0)
                wait_alone(dve, pad_clear, 2 * (b + 1))
                with dve.Fori(1, NWIN) as rr:
                    sums_row(b, rr)
                    dve.wait_ge(pad_evac, b * NWIN + rr + 1)
                    lepe_row(b * PER_IMAGE + SELF_A2 + (rr - 1) * LEPE_ROW, rr - 1)
                lepe_row(b * PER_IMAGE + SELF_A2 + (NWIN - 1) * LEPE_ROW, NWIN - 1)
                own[0] = SELF_A2 + NWIN * LEPE_ROW
                dve.wait_ge(affinity_done, b + 1)
                settle(dve.tensor_copy(affinity[:], bank[7][0:NREG, 0:NREG]), base)
                settle(dve.max(top[:], affinity[:]), base)
                dve.max_index(top_idx[:], top[:], affinity[:]).then_inc(top_done, 1)
                regions(b, 0, True)
                with dve.Fori(1, NWIN) as rr:
                    regions(b, rr, False)
                out_row(b * NWIN + NWIN - 1)

        @block.tensor
        def _(pe):
            pe.wait_ge(weights_in, 16 * N_WEIGHTS)
            pe.wait_ge(zeros_done, 2)

            def project(dst, col, rr, done):
                for k in range(KC):
                    last = pe.matmul(dst[:, 0:ROW], wqkv[:, k, col:col + P], xn[:, k, bass.ds(rr * ROW, ROW)],
                                     start=(k == 0), stop=(k == KC - 1))
                last.then_inc(done, 1)

            def out_row(g):
                pe.wait_ge(o_row_done, NWIN * (g + 1))
                for m in range(2):
                    for j in (2 * m, 2 * m + 1):
                        for k in range(KC):
                            last = pe.matmul(bank[2 + m][0:TT, C * (j % 2):C * (j % 2 + 1)],
                                             o_row[:, k, TT * j:TT * (j + 1)], wout[:, k, :],
                                             start=(k == 0), stop=(k == KC - 1))
                    last.then_inc(out_proj, 1)

            def scores(r, rc):
                pe.wait_ge(k_sel_done, r + 1)
                for p in range(PAIRS):
                    k, h = divmod(2 * p, HG)
                    pe.matmul(bank[p][:, 0:KEYS], q_blocks[:, k, rc, h:h + 2, :].rearrange("p h t -> p (h t)"),
                              k_sel[:, rc % 2, k, :], start=True, stop=True).then_inc(scores_done, 1)

            def turn_probs(r):
                pe.wait_ge(probs_t_evac, CH * r)
                for p in range(PAIRS):
                    pe.wait_ge(probs_done, PAIRS * r + p + 1)
                    for c in range(CH):
                        t = pe.transpose(bank[4 + c][:, P * p:P * (p + 1)], probs[:, p, P * c:P * (c + 1)], ident[:])
                        if p == PAIRS - 1:
                            t.then_inc(probs_turned, 1)

            def attend(g, r, rc):
                pe.wait_ge(probs_t_evac, CH * (r + 1))
                pe.wait_ge(v_sel_in[rc % 2], 16 * TOPK * slot_uses(g, rc))
                pe.wait_ge(o_row_done, r)
                for k in range(KC):
                    for c in range(CH):
                        for h in range(HG):
                            head = HG * k + h
                            last = pe.matmul(bank[6][HD * h:HD * (h + 1), RT * k:RT * (k + 1)],
                                             v_sel[:, rc % 2, c, HD * head:HD * (head + 1)],
                                             probs_t[:, c, RT * head:RT * (head + 1)],
                                             start=(c == 0), stop=(c == CH - 1))
                last.then_inc(attn_done, 1)

            def regions(b, rr, first):
                g = b * NWIN + rr
                for k in range(KC):
                    project(bank[k], P * k, rr, q_proj)
                if not first:
                    out_row(g - 1)
                pe.wait_ge(q_evac_act, g + 1)
                pe.wait_ge(q_evac_dve, g + 1)
                if not first:
                    pe.wait_ge(out_evac, 2 * g)
                scores(g * NWIN, 0)
                for rc in range(NWIN):
                    r = g * NWIN + rc
                    turn_probs(r)
                    if rc + 1 < NWIN:
                        scores(r + 1, rc + 1)
                    attend(g, r, rc)

            with pe.Fori(0, NB) as b:
                pe.wait_ge(x_in_done, 16 * (b + 1))
                pe.wait_ge(out_evac, 2 * NWIN * b)
                for t in range(NWIN):
                    for k in range(KC):
                        n = KC * t + k
                        if n >= 4:
                            pe.wait_ge(x_evac, KC * NWIN * b + n - 3)
                        for j in range(NT):
                            last = pe.transpose(bank[n % 4][:, TT * j:TT * (j + 1)],
                                                x_in[:, NT * t + j, P * k:P * (k + 1)], ident[0:TT, 0:TT])
                        last.then_inc(x_turned, 1)
                pe.wait_ge(mean_done, b + 1)
                pe.matmul(bank[4][:, 0:KC], group[:], mv[:, :, 0], start=True, stop=True).then_inc(mean_taken, 1)
                pe.wait_ge(var_done, b + 1)
                pe.matmul(bank[5][:, 0:KC], group[:], var2[:], start=True, stop=True).then_inc(var_ready, 1)
                pe.wait_ge(scale_ready, b + 1)
                wait_alone(pe, x_evac, KC * NWIN * (b + 1))
                with pe.Fori(0, NWIN) as rr:
                    g = b * NWIN + rr
                    pe.wait_ge(row_normed, KC * (g + 1))
                    pe.wait_ge(v_evac, KC * g)
                    for k in range(KC):
                        project(bank[2 + k], 2 * C + P * k, rr, v_proj)
                    pe.wait_ge(k_evac, KC * g)
                    for k in range(KC):
                        project(bank[k], C + P * k, rr, k_proj)
                    pe.wait_ge(v_evac, KC * (g + 1))
                    wait_alone(pe, v_tok_evac, 4 * g)
                    for reg in range(NWIN):
                        for k in range(KC):
                            at = C * (reg % 2) + P * k
                            last = pe.transpose(bank[4 + reg // 2][0:RT, at:at + P],
                                                v_row[:, k, RT * reg:RT * (reg + 1)], ident[:])
                        if reg % 2 or reg == NWIN - 1:
                            last.then_inc(v_turned, 1)
                pe.wait_ge(region_sums, NWIN * (b + 1))
                pe.wait_ge(k_evac, KC * NWIN * (b + 1))
                for m in range(2 * KC):
                    for k in range(KC):
                        last = pe.matmul(bank[0][:, NREG * m:NREG * (m + 1)], wqkv[:, k, P * m:P * (m + 1)],
                                         x_sum[:, k, :], start=(k == 0), stop=(k == KC - 1))
                last.then_inc(means_proj, 1)
                pe.wait_ge(means_evac, 2 * KC * (b + 1))
                pe.wait_ge(v_tok_evac, 4 * NWIN * (b + 1))
                for k in range(KC):
                    last = pe.matmul(bank[7][0:NREG, 0:NREG], qk_mean[:, k, :], qk_mean[:, KC + k, :],
                                     start=(k == 0), stop=(k == KC - 1))
                last.then_inc(affinity_done, 1)
                regions(b, 0, True)
                with pe.Fori(1, NWIN) as rr:
                    regions(b, rr, False)
                out_row(b * NWIN + NWIN - 1)


def kernel(x, L0_conv_qkv_w, L0_conv_qkv_b, L0_conv_lepe_w, L0_conv_lepe_b, L0_conv_out_w, L0_conv_out_b):
    import numpy as np
    import concourse.bacc as bacc
    from concourse.bass_utils import run_bass_kernel_spmd as run

    def chunked(a):
        a = np.asarray(a)
        return np.ascontiguousarray(np.moveaxis(a.reshape(-1, P, *a.shape[1:]), 0, 1))

    arrays = {
        "x": np.ascontiguousarray(np.asarray(x).reshape(NB * NWIN, ROW, C)),
        "w_qkv": np.ascontiguousarray(np.asarray(L0_conv_qkv_w).T),
        "w_out": np.ascontiguousarray(np.asarray(L0_conv_out_w).T),
        "b_qkv": chunked(L0_conv_qkv_b),
        "b_out": np.ascontiguousarray(np.broadcast_to(np.asarray(L0_conv_out_b), (TT, C))),
        "w_tap": chunked(np.asarray(L0_conv_lepe_w).reshape(C, TAPS)),
        "b_tap": chunked(L0_conv_lepe_b),
        "ident": np.eye(P, dtype=np.float32),
        "group": np.kron(np.eye(P // GROUP), np.full((GROUP, GROUP), 1.0 / GROUP)).astype(np.float32),
    }
    nc = bacc.Bacc("TRN2", target_bir_lowering=False, num_devices=1)
    args = [nc.dram_tensor(f"{n}_dram", list(a.shape), F32, kind="ExternalInput").ap() for n, a in arrays.items()]
    out = nc.dram_tensor("out_dram", [NB * NWIN, ROW, C], F32, kind="ExternalOutput").ap()
    attention_kernel(nc, *args, out)
    r = run(nc, [{f"{n}_dram": a for n, a in arrays.items()}], core_ids=[0])
    return r.results[0]["out_dram"].reshape(NB, H, W, C)
```

```python
from contextlib import ExitStack

import concourse.bass as bass
from concourse import mybir

F32 = mybir.dt.float32
U32 = mybir.dt.uint32
I32 = mybir.dt.int32
ALU = mybir.AluOpType
ACT = mybir.ActivationFunctionType
AX = mybir.AxisListType

P = 128
NB, H, W, C = 8, 56, 56, 256
HEADS, HD = 8, 32
NWIN, TOPK = 7, 4
RS = H // NWIN
RT = RS * RS
NREG = NWIN * NWIN
ROW = RS * W
TOK = H * W
KC = C // P
HG = P // HD
PAIRS = HEADS // 2
KEYS = TOPK * RT
CH = KEYS // P
TT = 2 * W
NT = ROW // TT
PADW = W + 2
GROUP = C // 32
EPS = 1e-5
SCALE = C ** -0.5
TAPS = 9
EARLY_TAPS = 3
LATE = KC * (TAPS - EARLY_TAPS)
X_TILES = KC * NWIN
X_AHEAD = 8
LAST_ROW_STEPS = (1, 1, 1, 1, 1, 3, 4)
IDX_BITS = 6
BY_DMA = (0, 1, 3)
BY_POOL = 2
SLOT = (0, 1, 0, 1, 0, 1, 2)
BACK = (3, 3, 2, 2, 2, 2, 7)
START = 2 * PAIRS + 1


def attention_kernel(nc, x, w_qkv, w_out, b_qkv, b_out, w_tap, b_tap, ident_d, group_d, out):
    x_rows = x.rearrange("g (j p) c -> g p j c", p=TT)
    out_rows = out.rearrange("g (j p) c -> g p j c", p=TT)
    x_img = x.rearrange("(b r) (j p) c -> b p (r j) c", b=NB, p=TT)

    with ExitStack() as ctx:
        def sb(name, shape, dt=F32):
            return ctx.enter_context(nc.sbuf_tensor(name, shape, dt))

        def sem(name):
            return ctx.enter_context(nc.semaphore(name))

        wqkv = sb("wqkv", [P, KC, 3 * C])
        wout = sb("wout", [P, KC, C])
        bqkv = sb("bqkv", [P, 3 * KC])
        bq_scaled = sb("bq_scaled", [P, KC])
        bout = sb("bout", [TT, C])
        taps = sb("taps", [P, KC, TAPS])
        btap = sb("btap", [P, KC])
        ident = sb("ident", [P, P])
        group = sb("group", [P, P])
        x_tok = sb("x_tok", [P, NWIN * NT * C])
        x_in = x_tok[0:TT, :].rearrange("p (t c) -> p t c", c=C)
        v_pad = x_tok[:, 0:KC * PADW * PADW].rearrange("p (k r c) -> p k r c", k=KC, r=PADW)
        xn = sb("xn", [P, KC, TOK])
        k_all = sb("k_all", [P, KC, TOK])
        v_tok = sb("v_tok", [RT, NREG, C])
        lepe = sb("lepe", [P, KC, TOK])
        q_blocks = sb("q_blocks", [P, KC, NWIN, HG, RT])
        o_row = sb("o_row", [P, KC, ROW])
        resid = sb("resid", [TT, NT, C])
        probs = sb("probs", [P, PAIRS, KEYS])
        v_row = probs[:, :, :].rearrange("p a b -> p (a b)")[:, 0:KC * ROW].rearrange("p (k t) -> p k t", k=KC)
        probs_t = sb("probs_t", [P, CH, HEADS * RT])
        k_sel = sb("k_sel", [P, len(set(SLOT)), KC, KEYS])
        v_sel = sb("v_sel", [P, len(set(SLOT)), CH, C])
        tap_products = [probs_t[:, :, 0:ROW],
                        k_sel[:, :, :, :].rearrange("p s k t -> p (s k t)")[:, 0:KC * ROW].rearrange(
                            "p (k t) -> p k t", k=KC)]
        neg_max = sb("neg_max", [P, PAIRS])
        denom = sb("denom", [P, PAIRS])
        rdenom = sb("rdenom", [P, PAIRS])
        stats = sb("stats", [P, KC, NWIN, 6])
        mv = sb("mv", [P, KC, 2])
        dev = sb("dev", [P, KC])
        var2 = sb("var2", [P, KC])
        rstd = sb("rstd", [P, KC])
        neg_half = sb("neg_half", [P, KC])
        shift = sb("shift", [P, KC])
        x_sum = sb("x_sum", [P, KC, NREG])
        qk_mean = sb("qk_mean", [P, 2 * KC, NREG])
        affinity = sb("affinity", [NREG, NREG])
        top = sb("top", [NREG, 8])
        top_idx = sb("top_idx", [NREG, 8], U32)
        packed_idx = sb("packed_idx", [NREG, TOPK], I32)
        idx_row = sb("idx_row", [1, NREG], I32)

        bank = [ctx.enter_context(nc.psum_tensor(f"bank{i}", [P, 512], F32)) for i in range(8)]

        weights_in, x_in_done, idx_in = sem("weights_in"), sem("x_in_done"), sem("idx_in")
        v_sel_done = sem("v_sel_done")
        v_sel_in = [sem(f"v_sel_in{i}") for i in range(len(set(SLOT)))]
        resid_in, out_stored = sem("resid_in"), sem("out_stored")
        waits_passed = sem("waits_passed")
        dve_self = sem("dve_self")
        setup_done, zeros_done = sem("setup_done"), sem("zeros_done")
        x_turned, x_evac, stats_done, mean_done, mean_taken, var_done = map(
            sem, ("x_turned", "x_evac", "stats_done", "mean_done", "mean_taken", "var_done"))
        var_ready, scale_ready, row_normed, region_sums = map(sem, ("var_ready", "scale_ready", "row_normed", "region_sums"))
        var_eps, rstd_ready = sem("var_eps"), sem("rstd_ready")
        v_proj, k_proj, v_evac, k_evac, v_turned, v_tok_evac, pad_clear, pad_evac = map(
            sem, ("v_proj", "k_proj", "v_evac", "k_evac", "v_turned", "v_tok_evac", "pad_clear", "pad_evac"))
        means_proj, means_evac, affinity_done, top_done, lepe_done = map(
            sem, ("means_proj", "means_evac", "affinity_done", "top_done", "lepe_done"))
        taps_done, taps_added, lepe_begun, tap_added = map(sem, ("taps_done", "taps_added", "lepe_begun", "tap_added"))
        q_proj, q_evac_act, q_evac_dve = sem("q_proj"), sem("q_evac_act"), sem("q_evac_dve")
        k_sel_done, scores_done, max_done, exp_done, probs_done = map(
            sem, ("k_sel_done", "scores_done", "max_done", "exp_done", "probs_done"))
        probs_turned, probs_t_evac, attn_done, o_row_done, out_proj, out_evac, resid_ready = map(
            sem, ("probs_turned", "probs_t_evac", "attn_done", "o_row_done", "out_proj", "out_evac", "resid_ready"))

        def by_region(flat):
            return flat.rearrange("p (g r c) -> p r g c", g=NWIN, r=RS)

        def by_image(flat):
            return flat.rearrange("p (r g c) -> p r g c", r=RS, g=NWIN)

        def q_block(s, k, h):
            return q_blocks[s, k, :, h, :].rearrange("p g (r c) -> p r g c", r=RS)

        def lepe_row(k, rr):
            return lepe[:, k, bass.ds(rr * ROW, ROW)].rearrange("p (r c) -> p r c", c=W)

        def tap_input(t, k, rr):
            return v_pad[:, k, bass.ds(rr * RS + t // 3, RS), t % 3:t % 3 + W]

        def slot_uses(g, rc):
            return g * SLOT.count(SLOT[rc]) + SLOT[:rc + 1].count(SLOT[rc])

        def before(r, rc):
            return r - BACK[rc] + 1

        N_WEIGHTS = 8

        def chosen(eng, rr, rc):
            word = eng.value_load(idx_row[0:1, bass.ds(rr * NWIN + rc, 1)])
            return [nc.s_assert_within((word >> (IDX_BITS * j)) & (2 ** IDX_BITS - 1), 0, NREG - 1,
                                       skip_runtime_bounds_check_because="max_index gives one of the 49 regions")
                    for j in range(TOPK)]

        def wait_alone(eng, semaphore, value):
            eng.wait_ge(semaphore, value)
            eng.sem_inc(waits_passed, 1)

        block = ctx.enter_context(nc.Block())

        @block.sync
        def _(sp):
            sp.dma_start(x_in, x_img[0]).then_inc(x_in_done, 16)
            sp.dma_start(ident[:], ident_d).then_inc(weights_in, 16)
            sp.dma_start(group[:], group_d).then_inc(weights_in, 16)
            sp.dma_start(wqkv[:], w_qkv.rearrange("(k p) o -> p k o", p=P)).then_inc(weights_in, 16)
            sp.dma_start(bqkv[:], b_qkv).then_inc(weights_in, 16)
            sp.dma_start(taps[:], w_tap).then_inc(weights_in, 16)
            sp.dma_start(btap[:], b_tap).then_inc(weights_in, 16)
            sp.dma_start(wout[:], w_out.rearrange("(k p) o -> p k o", p=P)).then_inc(weights_in, 16)
            sp.dma_start(bout[:], b_out).then_inc(weights_in, 16)

            sp.sem_inc(out_stored, START)

            def store_row(g):
                sp.wait_ge(out_evac, START + 2 * g + 2)
                sp.dma_start(out_rows[g], resid[:]).then_inc(out_stored, 16)

            def regions(b, rr, first):
                g = b * NWIN + rr
                for rc in range(NWIN):
                    r = g * NWIN + rc
                    reg = chosen(sp, rr, rc)
                    wait_alone(sp, attn_done, START + before(r, rc))
                    for j in BY_DMA:
                        half = RT * (j % 2)
                        sp.dma_start(v_sel[half:half + RT, SLOT[rc], j // 2, :],
                                     v_tok[:, bass.ds(reg[j], 1), :]).then_inc(v_sel_in[SLOT[rc]], 16)
                    if rc == 2 and not first:
                        store_row(g - 1)
                    if rc == 4:
                        sp.wait_ge(out_stored, START + 16 * g)
                        sp.dma_start(resid[:], x_rows[g]).then_inc(resid_in, 16)

            def image(b, last):
                sp.wait_ge(top_done, b + 1)
                sp.dma_start(idx_row[:], packed_idx[:, 0:1]).then_inc(idx_in, 16)
                wait_alone(sp, idx_in, 16 * (b + 1))
                wait_alone(sp, v_tok_evac, START + 4 * NWIN * (b + 1))
                regions(b, 0, True)
                with sp.Fori(1, NWIN - 1) as rr:
                    regions(b, rr, False)
                if not last:
                    sp.wait_ge(lepe_done, NWIN * (b + 1))
                    sp.dma_start(x_in, x_img[b + 1]).then_inc(x_in_done, 16)
                regions(b, NWIN - 1, False)
                store_row(b * NWIN + NWIN - 1)

            with sp.Fori(0, NB - 1) as b:
                image(b, False)
            image(NB - 1, True)
            sp.wait_ge(out_stored, START + 16 * NB * NWIN)

        @block.gpsimd
        def _(pool):
            pool.memset(neg_half[:], -0.5).then_inc(zeros_done, 1)
            pool.memset(q_blocks[:, :, :, :, :], 0.0).then_inc(zeros_done, 1)

            def add_bias(g):
                pool.wait_ge(resid_in, 16 * (g + 1))
                pool.tensor_tensor(resid[:], resid[:], bout[:, :].unsqueeze(1).to_broadcast([TT, NT, C]),
                                   ALU.add).then_inc(resid_ready, 1)

            def gather_keys(r, rc, reg):
                pool.wait_ge(scores_done, START + PAIRS * before(r, rc))
                for j in range(TOPK):
                    last = pool.tensor_copy(k_sel[:, SLOT[rc], :, RT * j:RT * (j + 1)],
                                            k_all[:, :, bass.ds(reg[j] * RT, RT)])
                last.then_inc(k_sel_done, 1)

            def gather_values(r, rc, reg):
                pool.wait_ge(attn_done, START + before(r, rc))
                pool.tensor_copy(v_sel[0:RT, SLOT[rc], 1, :],
                                 v_tok[:, bass.ds(reg[BY_POOL], 1), :].rearrange("p n c -> p (n c)")
                                 ).then_inc(v_sel_done, 1)

            def regions(b, rr):
                g = b * NWIN + rr
                reg = None
                for rc in range(NWIN):
                    reg, reg_before = chosen(pool, rr, rc), reg
                    gather_keys(g * NWIN + rc, rc, reg)
                    if rc:
                        gather_values(g * NWIN + rc - 1, rc - 1, reg_before)
                gather_values(g * NWIN + NWIN - 1, NWIN - 1, reg)
                add_bias(g)

            def add_taps(g, rr, is_last=False):
                wait_alone(pool, pad_evac, START + g + (1 if is_last else 2))
                wait_alone(pool, lepe_begun, START + g)
                for k in range(KC):
                    last = pool.tensor_tensor(tap_products[1][:, k, :].rearrange("p (r c) -> p r c", c=W),
                                              tap_input(2, k, rr),
                                              taps[:, k, 2:3].unsqueeze(2).to_broadcast([P, RS, W]), ALU.mult)
                last.then_inc(taps_added, 1)
                row = lepe[:, :, bass.ds(rr * ROW, ROW)]
                wait_alone(pool, taps_done, g + 1)
                pool.tensor_tensor(row, row, tap_products[0], ALU.add).then_inc(taps_added, 1)
                wait_alone(pool, taps_added, 2 * (g + 1))
                pool.tensor_tensor(row, row, tap_products[1], ALU.add).then_inc(lepe_begun, 1)

            pool.sem_inc(lepe_begun, START)
            pool.wait_ge(weights_in, 16 * N_WEIGHTS)
            with pool.Fori(0, NB) as b:
                pool.wait_ge(zeros_done, 2)
                pool.wait_ge(var_eps, b + 1)
                pool.tensor_tensor(rstd[:], var2[:], neg_half[:], ALU.pow).then_inc(rstd_ready, 1)
                wait_alone(pool, x_turned, KC * NWIN * (b + 1))
                pool.memset(v_pad[:, :, 0:PADW:PADW - 1, :], 0.0).then_inc(pad_clear, 1)
                pool.memset(v_pad[:, :, 1:PADW - 1, 0:PADW:PADW - 1], 0.0).then_inc(pad_clear, 1)
                wait_alone(pool, pad_clear, 2 * (b + 1))
                with pool.Fori(0, NWIN - 1) as rr:
                    add_taps(b * NWIN + rr, rr)
                add_taps(b * NWIN + NWIN - 1, NWIN - 1, True)
                wait_alone(pool, lepe_begun, START + NWIN * (b + 1))
                pool.wait_ge(idx_in, 16 * (b + 1))
                wait_alone(pool, k_evac, START + KC * NWIN * (b + 1))
                with pool.Fori(0, NWIN) as rr:
                    regions(b, rr)

        @block.scalar
        def _(act):
            act.wait_ge(weights_in, 16 * N_WEIGHTS)
            act.wait_ge(setup_done, 1)

            for s in (x_evac, pad_evac, k_evac, v_tok_evac, probs_t_evac):
                act.sem_inc(s, START)

            def normalize(rr):
                for k in range(KC):
                    act.activation(xn[:, k, bass.ds(rr * ROW, ROW)], xn[:, k, bass.ds(rr * ROW, ROW)], ACT.Identity,
                                   bias=shift[:, k:k + 1], scale=rstd[:, k:k + 1]).then_inc(row_normed, 1)

            def multiply_taps(g, rr, is_last=False):
                act.wait_ge(pad_evac, START + g + (1 if is_last else 2))
                act.wait_ge(lepe_begun, START + g)
                for k in range(KC):
                    act.activation(lepe_row(k, rr), tap_input(0, k, rr), ACT.Identity,
                                   bias=btap[:, k:k + 1], scale=taps[:, k, 0:1])
                    last = act.activation(tap_products[0][:, k, :].rearrange("p (r c) -> p r c", c=W),
                                          tap_input(1, k, rr), ACT.Copy, scale=taps[:, k, 1:2])
                last.then_inc(taps_done, 1)

            def qkv_row(b, rr, first, last):
                g = b * NWIN + rr
                act.wait_ge(v_turned, START + 4 * g)
                for k in range(KC):
                    act.wait_ge(v_proj, KC * g + k + 1)
                    act.activation(by_region(v_row[:, k, :]), by_image(bank[2 + k][:, 0:ROW]), ACT.Identity,
                                   bias=bqkv[:, 2 * KC + k:2 * KC + k + 1]).then_inc(v_evac, 1)
                    ins = act.activation(v_pad[:, k, bass.ds(rr * RS + 1, RS), 1:1 + W],
                                         bank[2 + k][:, 0:ROW].rearrange("p (r c) -> p r c", c=W), ACT.Identity,
                                         bias=bqkv[:, 2 * KC + k:2 * KC + k + 1])
                ins.then_inc(pad_evac, 1)
                for k in range(KC):
                    act.wait_ge(k_proj, KC * g + k + 1)
                    act.activation(by_region(k_all[:, k, bass.ds(rr * ROW, ROW)]), by_image(bank[k][:, 0:ROW]),
                                   ACT.Identity, bias=bqkv[:, KC + k:KC + k + 1]).then_inc(k_evac, 1)
                if not last:
                    normalize(rr + 1)
                if not first:
                    multiply_taps(g - 1, rr - 1)
                for m in range(4):
                    act.wait_ge(v_turned, START + 4 * g + m + 1)
                    n = min(2, NWIN - 2 * m)
                    act.copy(v_tok[:, bass.ds(rr * NWIN + 2 * m, n), :],
                             bank[4 + m][0:RT, 0:n * C].rearrange("p (n c) -> p n c", n=n)).then_inc(v_tok_evac, 1)

            def q_evac(g, k):
                act.wait_ge(q_proj, KC * g + k + 1)
                for h in range(HG // 2):
                    s = slice(HD * h, HD * (h + 1))
                    last = act.activation(q_block(s, k, h), by_image(bank[7][s, 0:ROW]), ACT.Identity,
                                          bias=bq_scaled[s, k:k + 1], scale=SCALE)
                last.then_inc(q_evac_act, 1)

            def probs_t_out(r, k):
                act.wait_ge(probs_turned, KC * r + k + 1)
                if k == 0:
                    act.wait_ge(attn_done, START + r)
                act.copy(probs_t[:, k, :], bank[4 + k][:, :]).then_inc(probs_t_evac, 1)

            def exp(r, p):
                act.wait_ge(max_done, PAIRS * r + p + 1)
                act.activation(probs[:, p, :], bank[p][:, 0:KEYS], ACT.Exp, bias=neg_max[:, p:p + 1],
                               accum_out=denom[:, p:p + 1]).then_inc(exp_done, 1)

            def regions(b, rr, last):
                g = b * NWIN + rr
                for rc in range(NWIN):
                    r = g * NWIN + rc
                    more = not (last and rc == NWIN - 1)
                    if more:
                        exp(r + 1, 0)
                    if rc == NWIN - 1 and not last:
                        q_evac(g + 1, 1)
                    if more:
                        exp(r + 1, 1)
                    probs_t_out(r, 0)
                    if rc == NWIN - 2 and not last:
                        q_evac(g + 1, 0)
                    probs_t_out(r, 1)
                    if more:
                        exp(r + 1, 2)
                        exp(r + 1, 3)

            def x_out(b):
                for n in range(X_TILES):
                    t, k = divmod(n, KC)
                    act.wait_ge(x_turned, X_TILES * b + n + 1)
                    act.copy(xn[:, k, ROW * t:ROW * (t + 1)], bank[n % 4][:, 0:ROW]).then_inc(x_evac, 1)

            def image(b, last):
                act.wait_ge(scale_ready, b + 1)
                wait_alone(act, pad_clear, 2 * (b + 1))
                normalize(0)
                qkv_row(b, 0, True, False)
                with act.Fori(1, NWIN - 1) as rr:
                    qkv_row(b, rr, False, False)
                qkv_row(b, NWIN - 1, False, True)
                act.wait_ge(means_proj, b + 1)
                for m in range(2 * KC):
                    act.activation(qk_mean[:, m, :], bank[0][:, NREG * m:NREG * (m + 1)], ACT.Identity,
                                   bias=bqkv[:, m:m + 1], scale=1.0 / RT).then_inc(means_evac, 1)
                multiply_taps(b * NWIN + NWIN - 1, NWIN - 1, True)
                for k in range(KC):
                    q_evac(b * NWIN, k)
                for p in range(PAIRS):
                    exp(b * NREG, p)
                with act.Fori(0, NWIN - 1) as rr:
                    regions(b, rr, False)
                regions(b, NWIN - 1, True)
                if not last:
                    x_out(b + 1)

            x_out(0)
            with act.Fori(0, NB - 1) as b:
                image(b, False)
            image(NB - 1, True)

        @block.vector
        def _(dve):
            own = [0]

            def settle(ins, base):
                own[0] += 1
                ins.then_inc(dve_self, 1)
                wait_alone(dve, dve_self, base + own[0])

            dve.wait_ge(weights_in, 16 * N_WEIGHTS)
            dve.tensor_scalar(bq_scaled[:], bqkv[:, 0:KC], SCALE, None, ALU.mult).then_inc(setup_done, 1)

            PER_REGION = PAIRS
            SELF_A2 = 2
            SELF_TOP = 5
            IN_B = SELF_A2 + SELF_TOP
            PER_IMAGE = IN_B + NREG * PER_REGION

            def add_late_taps(g, rr, steps=range(LATE)):
                for i in steps:
                    t, k = EARLY_TAPS + i // KC, i % KC
                    if i == 0:
                        dve.wait_ge(lepe_begun, START + g + 1)
                    if i >= KC:
                        dve.wait_ge(tap_added, (LATE - KC) * g + i - KC + 1)
                    ins = dve.scalar_tensor_tensor(lepe_row(k, rr), tap_input(t, k, rr), taps[:, k, t:t + 1],
                                                   lepe_row(k, rr), ALU.mult, ALU.add)
                    if i < LATE - KC:
                        ins.then_inc(tap_added, 1)
                    elif i == LATE - 1:
                        ins.then_inc(lepe_done, 1)

            def sums_row(b, rr):
                dve.wait_ge(row_normed, KC * (b * NWIN + rr + 1))
                for k in range(KC):
                    ins = dve.tensor_reduce(
                        x_sum[:, k, bass.ds(rr * NWIN, NWIN)],
                        xn[:, k, bass.ds(rr * ROW, ROW)].rearrange("p (r g c) -> p g r c", r=RS, g=NWIN), AX.XY, ALU.add)
                ins.then_inc(region_sums, 1)

            for s in (out_evac, o_row_done):
                dve.sem_inc(s, START)

            def q_evac(g, k):
                dve.wait_ge(q_proj, KC * g + k + 1)
                for h in range(HG // 2, HG):
                    s = slice(HD * h, HD * (h + 1))
                    last = dve.tensor_scalar(q_block(s, k, h), by_image(bank[7][s, 0:ROW]), SCALE,
                                             bq_scaled[s, k:k + 1], ALU.mult, ALU.add)
                last.then_inc(q_evac_dve, 1)

            def out_half(g, m):
                if m == 0:
                    dve.wait_ge(resid_ready, g + 1)
                dve.wait_ge(out_proj, 2 * g + m + 1)
                dve.tensor_tensor(resid[:, 2 * m:2 * m + 2, :],
                                  bank[7][0:TT, :].rearrange("p (j c) -> p j c", j=2),
                                  resid[:, 2 * m:2 * m + 2, :], ALU.add).then_inc(out_evac, 1)

            def maximum(r, p):
                dve.wait_ge(scores_done, START + PAIRS * r + p + 1)
                dve.tensor_reduce(neg_max[:, p:p + 1], bank[p][:, 0:KEYS], AX.X, ALU.max,
                                  negate=True).then_inc(max_done, 1)

            def invert(r, p):
                dve.wait_ge(exp_done, PAIRS * r + p + 1)
                dve.reciprocal(rdenom[:, p:p + 1], denom[:, p:p + 1]).then_inc(dve_self, 1)

            def divide(p, base):
                dve.wait_ge(dve_self, base + p + 1)
                dve.tensor_scalar(probs[:, p, :], probs[:, p, :], rdenom[:, p:p + 1], None,
                                  ALU.mult).then_inc(probs_done, 1)

            def take_region(r, rr, rc):
                dve.wait_ge(attn_done, START + r + 1)
                cols = slice(RS * rc, RS * (rc + 1))
                dve.tensor_tensor(o_row[:, :, :].rearrange("p k (r c) -> p k r c", c=W)[:, :, :, cols],
                                  bank[6][:, 0:KC * RT].rearrange("p (k r c) -> p k r c", k=KC, r=RS),
                                  lepe[:, :, bass.ds(rr * ROW, ROW)].rearrange("p k (r c) -> p k r c", c=W)[:, :, :, cols],
                                  ALU.add).then_inc(o_row_done, 1)

            def normalized(r, p, base):
                invert(r, p)
                divide(p, base)

            def regions(b, rr, first, last):
                g = b * NWIN + rr
                for rc in range(NWIN):
                    r = g * NWIN + rc
                    base = b * PER_IMAGE + IN_B + (rr * NWIN + rc) * PER_REGION
                    more = not (last and rc == NWIN - 1)
                    if more:
                        maximum(r + 1, 0)
                    normalized(r, 2, base)
                    if rc == 1 and not first:
                        out_half(g - 1, 1)
                    if rc == NWIN - 1 and not last:
                        q_evac(g + 1, 1)
                    if more:
                        maximum(r + 1, 1)
                    normalized(r, 3, base)
                    if more:
                        normalized(r + 1, 0, base + PER_REGION)
                    if rc:
                        take_region(r - 1, rr, rc - 1)
                    elif not first:
                        take_region(r - 1, rr - 1, NWIN - 1)
                    if first:
                        done = sum(LAST_ROW_STEPS[:rc])
                        add_late_taps(b * NWIN + NWIN - 1, NWIN - 1, range(done, done + LAST_ROW_STEPS[rc]))
                    if rc == NWIN - 2 and not last:
                        q_evac(g + 1, 0)
                    if more:
                        maximum(r + 1, 2)
                    if rc == 0 and not first:
                        out_half(g - 1, 0)
                    if more:
                        normalized(r + 1, 1, base + PER_REGION)
                        maximum(r + 1, 3)

            def x_stats(b, tiles):
                for n in tiles:
                    t, k = divmod(n, KC)
                    dve.wait_ge(x_evac, START + X_TILES * b + n + 1)
                    ins = dve.bn_stats(stats[:, k, t, :], xn[:, k, ROW * t:ROW * (t + 1)])
                    if n == X_TILES - 1:
                        ins.then_inc(stats_done, 1)

            def image(b, is_last):
                wait_alone(dve, stats_done, b + 1)
                own[0] = 0
                base = b * PER_IMAGE
                for k in range(KC):
                    last = dve.bn_aggr(mv[:, k, :], stats[:, k, :, :])
                last.then_inc(mean_done, 1)
                dve.wait_ge(mean_taken, b + 1)
                settle(dve.tensor_tensor(dev[:], mv[:, :, 0], bank[4][:, 0:KC], ALU.subtract), base)
                settle(dve.tensor_tensor(dev[:], dev[:], dev[:], ALU.mult), base)
                dve.tensor_tensor(var2[:], dev[:], mv[:, :, 1], ALU.add).then_inc(var_done, 1)
                dve.wait_ge(var_ready, b + 1)
                dve.tensor_scalar(var2[:], bank[5][:, 0:KC], EPS, None, ALU.add).then_inc(var_eps, 1)
                dve.wait_ge(rstd_ready, b + 1)
                dve.scalar_tensor_tensor(shift[:], bank[4][:, 0:KC], -1.0, rstd[:], ALU.mult,
                                         ALU.mult).then_inc(scale_ready, 1)
                sums_row(b, 0)
                sums_row(b, 1)
                with dve.Fori(1, NWIN - 1) as rr:
                    sums_row(b, rr + 1)
                    add_late_taps(b * NWIN + rr - 1, rr - 1)
                own[0] = SELF_A2
                dve.wait_ge(affinity_done, b + 1)
                settle(dve.tensor_copy(affinity[:], bank[6][0:NREG, 0:NREG]), base)
                settle(dve.max(top[:], affinity[:]), base)
                settle(dve.max_index(top_idx[:], top[:], affinity[:]), base)
                word = top_idx[:, TOPK - 1:TOPK]
                for j in range(TOPK - 2, -1, -1):
                    ins = dve.scalar_tensor_tensor(packed_idx[:, j:j + 1], word, float(2 ** IDX_BITS),
                                                   top_idx[:, j:j + 1], ALU.mult, ALU.add)
                    word = packed_idx[:, j:j + 1]
                    if j:
                        settle(ins, base)
                    else:
                        ins.then_inc(top_done, 1)
                for k in range(KC):
                    q_evac(b * NWIN, k)
                    add_late_taps(b * NWIN + NWIN - 2, NWIN - 2, range(LATE * k // KC, LATE * (k + 1) // KC))
                for p in range(PAIRS):
                    maximum(b * NREG, p)
                for p in range(2):
                    normalized(b * NREG, p, base + IN_B)
                regions(b, 0, True, False)
                with dve.Fori(1, NWIN - 1) as rr:
                    regions(b, rr, False, False)
                regions(b, NWIN - 1, False, True)
                if not is_last:
                    x_stats(b + 1, range(X_AHEAD))
                take_region(b * NREG + NREG - 1, NWIN - 1, NWIN - 1)
                if not is_last:
                    x_stats(b + 1, range(X_AHEAD, X_TILES))
                for m in range(2):
                    out_half(b * NWIN + NWIN - 1, m)

            x_stats(0, range(X_TILES))
            with dve.Fori(0, NB - 1) as b:
                image(b, False)
            image(NB - 1, True)

        @block.tensor
        def _(pe):
            pe.wait_ge(weights_in, 16 * N_WEIGHTS)
            pe.wait_ge(zeros_done, 2)

            def project(dst, col, rr, done):
                for k in range(KC):
                    last = pe.matmul(dst[:, 0:ROW], wqkv[:, k, col:col + P], xn[:, k, bass.ds(rr * ROW, ROW)],
                                     start=(k == 0), stop=(k == KC - 1))
                last.then_inc(done, 1)

            for s in (scores_done, attn_done, v_turned):
                pe.sem_inc(s, START)

            def project_q(g, rr, k):
                if k:
                    pe.wait_ge(q_evac_act, KC * g + 1)
                    pe.wait_ge(q_evac_dve, KC * g + 1)
                else:
                    pe.wait_ge(out_evac, START + 2 * (g - 1))
                project(bank[7], P * k, rr, q_proj)

            def out_half(g, m):
                if m == 0:
                    pe.wait_ge(o_row_done, START + NWIN * (g + 1))
                pe.wait_ge(out_evac, START + 2 * g + m)
                for j in (2 * m, 2 * m + 1):
                    for k in range(KC):
                        last = pe.matmul(bank[7][0:TT, C * (j % 2):C * (j % 2 + 1)],
                                         o_row[:, k, TT * j:TT * (j + 1)], wout[:, k, :],
                                         start=(k == 0), stop=(k == KC - 1))
                last.then_inc(out_proj, 1)

            def scores(r, g, rc, p):
                k, h = divmod(2 * p, HG)
                if p == 0:
                    pe.wait_ge(k_sel_done, r + 1)
                if rc == 0 and h == 0:
                    pe.wait_ge(q_evac_act, KC * g + k + 1)
                    pe.wait_ge(q_evac_dve, KC * g + k + 1)
                pe.matmul(bank[p][:, 0:KEYS], q_blocks[:, k, rc, h:h + 2, :].rearrange("p h t -> p (h t)"),
                          k_sel[:, SLOT[rc], k, :], start=True, stop=True).then_inc(scores_done, 1)

            def turn_probs(r, p):
                k = p // 2
                if p % 2 == 0:
                    pe.wait_ge(probs_t_evac, START + KC * (r - 1) + k + 1)
                pe.wait_ge(probs_done, PAIRS * r + p + 1)
                for c in range(CH):
                    at = P * (CH * (p % 2) + c)
                    t = pe.transpose(bank[4 + k][:, at:at + P], probs[:, p, P * c:P * (c + 1)], ident[:])
                if p % 2:
                    t.then_inc(probs_turned, 1)

            def attend(g, r, rc):
                pe.wait_ge(v_sel_in[SLOT[rc]], 16 * len(BY_DMA) * slot_uses(g, rc))
                pe.wait_ge(v_sel_done, r + 1)
                pe.wait_ge(o_row_done, START + r)
                for k in range(KC):
                    pe.wait_ge(probs_t_evac, START + KC * r + k + 1)
                    for c in range(CH):
                        for h in range(HG):
                            head = HG * k + h
                            at = RT * (2 * CH * (h // 2) + 2 * c + h % 2)
                            last = pe.matmul(bank[6][HD * h:HD * (h + 1), RT * k:RT * (k + 1)],
                                             v_sel[:, SLOT[rc], c, HD * head:HD * (head + 1)],
                                             probs_t[:, k, at:at + RT],
                                             start=(c == 0), stop=(c == CH - 1))
                last.then_inc(attn_done, 1)

            def regions(b, rr, first, last):
                g = b * NWIN + rr
                for rc in range(NWIN):
                    r = g * NWIN + rc
                    for p in range(PAIRS):
                        turn_probs(r, p)
                        if rc + 1 < NWIN:
                            scores(r + 1, g, rc + 1, p)
                        elif not last:
                            scores(r + 1, g + 1, 0, p)
                        if p == 0 and rc == 1 and not first:
                            out_half(g - 1, 1)
                        if p == 0 and rc == NWIN - 1 and not last:
                            project_q(g + 1, rr + 1, 1)
                        if p == 1 and rc:
                            attend(g, r - 1, rc - 1)
                        elif p == 1 and not first:
                            attend(g - 1, r - 1, NWIN - 1)
                        if p == 1 and rc == NWIN - 2 and not last:
                            project_q(g + 1, rr + 1, 0)
                        if p == 2 and rc == 0 and not first:
                            out_half(g - 1, 0)

            def turn_x(b, tiles):
                for n in tiles:
                    t, k = divmod(n, KC)
                    if n == 0:
                        pe.wait_ge(x_in_done, 16 * (b + 1))
                    if n >= 4:
                        pe.wait_ge(x_evac, START + X_TILES * b + n - 3)
                    for j in range(NT):
                        last = pe.transpose(bank[n % 4][:, TT * j:TT * (j + 1)],
                                            x_in[:, NT * t + j, P * k:P * (k + 1)], ident[0:TT, 0:TT])
                    last.then_inc(x_turned, 1)

            def image(b, is_last):
                pe.wait_ge(mean_done, b + 1)
                pe.matmul(bank[4][:, 0:KC], group[:], mv[:, :, 0], start=True, stop=True).then_inc(mean_taken, 1)
                pe.wait_ge(var_done, b + 1)
                pe.matmul(bank[5][:, 0:KC], group[:], var2[:], start=True, stop=True).then_inc(var_ready, 1)
                pe.wait_ge(scale_ready, b + 1)
                wait_alone(pe, x_evac, START + KC * NWIN * (b + 1))
                with pe.Fori(0, NWIN) as rr:
                    g = b * NWIN + rr
                    pe.wait_ge(row_normed, KC * (g + 1))
                    pe.wait_ge(pad_evac, START + g)
                    for k in range(KC):
                        project(bank[2 + k], 2 * C + P * k, rr, v_proj)
                    pe.wait_ge(k_evac, START + KC * g)
                    for k in range(KC):
                        project(bank[k], C + P * k, rr, k_proj)
                    pe.wait_ge(v_evac, KC * (g + 1))
                    wait_alone(pe, v_tok_evac, START + 4 * g)
                    for reg in range(NWIN):
                        for k in range(KC):
                            at = C * (reg % 2) + P * k
                            last = pe.transpose(bank[4 + reg // 2][0:RT, at:at + P],
                                                v_row[:, k, RT * reg:RT * (reg + 1)], ident[:])
                        if reg % 2 or reg == NWIN - 1:
                            last.then_inc(v_turned, 1)
                pe.wait_ge(region_sums, NWIN * (b + 1))
                pe.wait_ge(k_evac, START + KC * NWIN * (b + 1))
                for m in range(2 * KC):
                    for k in range(KC):
                        last = pe.matmul(bank[0][:, NREG * m:NREG * (m + 1)], wqkv[:, k, P * m:P * (m + 1)],
                                         x_sum[:, k, :], start=(k == 0), stop=(k == KC - 1))
                last.then_inc(means_proj, 1)
                pe.wait_ge(v_tok_evac, START + 4 * NWIN * (b + 1))
                project_q(b * NWIN, 0, 0)
                pe.wait_ge(means_evac, 2 * KC * (b + 1))
                for k in range(KC):
                    last = pe.matmul(bank[6][0:NREG, 0:NREG], qk_mean[:, k, :], qk_mean[:, KC + k, :],
                                     start=(k == 0), stop=(k == KC - 1))
                last.then_inc(affinity_done, 1)
                project_q(b * NWIN, 0, 1)
                for p in range(PAIRS):
                    scores(b * NREG, b * NWIN, 0, p)
                regions(b, 0, True, False)
                with pe.Fori(1, NWIN - 1) as rr:
                    regions(b, rr, False, False)
                regions(b, NWIN - 1, False, True)
                if not is_last:
                    turn_x(b + 1, range(X_AHEAD))
                attend(b * NWIN + NWIN - 1, b * NREG + NREG - 1, NWIN - 1)
                if not is_last:
                    turn_x(b + 1, range(X_AHEAD, X_TILES))
                for m in range(2):
                    out_half(b * NWIN + NWIN - 1, m)

            turn_x(0, range(X_TILES))
            with pe.Fori(0, NB - 1) as b:
                image(b, False)
            image(NB - 1, True)


def kernel(x, L0_conv_qkv_w, L0_conv_qkv_b, L0_conv_lepe_w, L0_conv_lepe_b, L0_conv_out_w, L0_conv_out_b):
    import numpy as np
    import concourse.bacc as bacc
    from concourse.bass_utils import run_bass_kernel_spmd as run

    def chunked(a):
        a = np.asarray(a)
        return np.ascontiguousarray(np.moveaxis(a.reshape(-1, P, *a.shape[1:]), 0, 1))

    arrays = {
        "x": np.ascontiguousarray(np.asarray(x).reshape(NB * NWIN, ROW, C)),
        "w_qkv": np.ascontiguousarray(np.asarray(L0_conv_qkv_w).T),
        "w_out": np.ascontiguousarray(np.asarray(L0_conv_out_w).T),
        "b_qkv": chunked(L0_conv_qkv_b),
        "b_out": np.ascontiguousarray(np.broadcast_to(np.asarray(L0_conv_out_b), (TT, C))),
        "w_tap": chunked(np.asarray(L0_conv_lepe_w).reshape(C, TAPS)),
        "b_tap": chunked(L0_conv_lepe_b),
        "ident": np.eye(P, dtype=np.float32),
        "group": np.kron(np.eye(P // GROUP), np.full((GROUP, GROUP), 1.0 / GROUP)).astype(np.float32),
    }
    nc = bacc.Bacc("TRN2", target_bir_lowering=False, num_devices=1)
    args = [nc.dram_tensor(f"{n}_dram", list(a.shape), F32, kind="ExternalInput").ap() for n, a in arrays.items()]
    out = nc.dram_tensor("out_dram", [NB * NWIN, ROW, C], F32, kind="ExternalOutput").ap()
    attention_kernel(nc, *args, out)
    r = run(nc, [{f"{n}_dram": a for n, a in arrays.items()}], core_ids=[0])
    return r.results[0]["out_dram"].reshape(NB, H, W, C)
```

```python
from contextlib import ExitStack

import concourse.bass as bass
from concourse import mybir

F32 = mybir.dt.float32
U32 = mybir.dt.uint32
I32 = mybir.dt.int32
ALU = mybir.AluOpType
ACT = mybir.ActivationFunctionType
AX = mybir.AxisListType

P = 128
NB, H, W, C = 8, 56, 56, 256
HEADS, HD = 8, 32
NWIN, TOPK = 7, 4
RS = H // NWIN
RT = RS * RS
NREG = NWIN * NWIN
ROW = RS * W
TOK = H * W
KC = C // P
HG = P // HD
PAIRS = HEADS // 2
KEYS = TOPK * RT
CH = KEYS // P
TT = 2 * W
NT = ROW // TT
PADW = W + 2
GROUP = C // 32
EPS = 1e-5
SCALE = C ** -0.5
TAPS = 9
EARLY_TAPS = 3
LATE = KC * (TAPS - EARLY_TAPS)
X_TILES = KC * NWIN
X_AHEAD = 8
IN_A = 6
STEPS = (2, 2, 0, 0, 0, 1, 1)
STEPS_ROW_0 = (1, 1, 1, 1, 0, 1, 1)
STEPS_OF_LAST = (1, 1, 1, 0, 1, 1, 1)
IDX_BITS = 6
BY_DMA = (0, 1, 3)
BY_POOL = 2
SLOT = (0, 1, 0, 1, 0, 1, 2)
BACK = (3, 3, 2, 2, 2, 2, 7)
START = 2 * PAIRS + 1


def attention_kernel(nc, x, w_qkv, w_out, b_qkv, b_out, w_tap, b_tap, ident_d, group_d, out):
    x_rows = x.rearrange("g (j p) c -> g p j c", p=TT)
    out_rows = out.rearrange("g (j p) c -> g p j c", p=TT)
    x_img = x.rearrange("(b r) (j p) c -> b p (r j) c", b=NB, p=TT)

    with ExitStack() as ctx:
        def sb(name, shape, dt=F32):
            return ctx.enter_context(nc.sbuf_tensor(name, shape, dt))

        def sem(name):
            return ctx.enter_context(nc.semaphore(name))

        wqkv = sb("wqkv", [P, KC, 3 * C])
        wout = sb("wout", [P, KC, C])
        bqkv = sb("bqkv", [P, 3 * KC])
        bq_scaled = sb("bq_scaled", [P, KC])
        bout = sb("bout", [TT, C])
        taps = sb("taps", [P, KC, TAPS])
        btap = sb("btap", [P, KC])
        ident = sb("ident", [P, P])
        group = sb("group", [P, P])
        x_tok = sb("x_tok", [P, NWIN * NT * C])
        x_in = x_tok[0:TT, :].rearrange("p (t c) -> p t c", c=C)
        v_pad = x_tok[:, 0:KC * PADW * PADW].rearrange("p (k r c) -> p k r c", k=KC, r=PADW)
        xn = sb("xn", [P, KC, TOK])
        k_all = sb("k_all", [P, KC, TOK])
        v_tok = sb("v_tok", [RT, NREG, C])
        lepe = sb("lepe", [P, KC, TOK])
        q_blocks = sb("q_blocks", [P, KC, NWIN, HG, RT])
        o_row = sb("o_row", [P, KC, ROW])
        resid = sb("resid", [TT, NT, C])
        probs = sb("probs", [P, PAIRS, KEYS])
        v_row = probs[:, :, :].rearrange("p a b -> p (a b)")[:, 0:KC * ROW].rearrange("p (k t) -> p k t", k=KC)
        probs_t = sb("probs_t", [P, CH, HEADS * RT])
        k_sel = sb("k_sel", [P, len(set(SLOT)), KC, KEYS])
        v_sel = sb("v_sel", [P, len(set(SLOT)), CH, C])
        tap_products = [probs_t[:, :, 0:ROW], o_row[:, :, :]]
        neg_max = sb("neg_max", [P, PAIRS])
        denom = sb("denom", [P, PAIRS])
        rdenom = sb("rdenom", [P, PAIRS])
        stats = sb("stats", [P, KC, NWIN, 6])
        mv = sb("mv", [P, KC, 2])
        dev = sb("dev", [P, KC])
        var2 = sb("var2", [P, KC])
        rstd = sb("rstd", [P, KC])
        neg_half = sb("neg_half", [P, KC])
        shift = sb("shift", [P, KC])
        x_sum = sb("x_sum", [P, KC, NREG])
        qk_mean = sb("qk_mean", [P, 2 * KC, NREG])
        affinity = sb("affinity", [NREG, NREG])
        top = sb("top", [NREG, 8])
        top_idx = sb("top_idx", [NREG, 8], U32)
        packed_idx = sb("packed_idx", [NREG, TOPK], I32)
        idx_row = sb("idx_row", [1, NREG], I32)

        bank = [ctx.enter_context(nc.psum_tensor(f"bank{i}", [P, 512], F32)) for i in range(8)]

        weights_in, x_in_done, idx_in = sem("weights_in"), sem("x_in_done"), sem("idx_in")
        v_sel_done = sem("v_sel_done")
        v_sel_in = [sem(f"v_sel_in{i}") for i in range(len(set(SLOT)))]
        resid_in, out_stored = sem("resid_in"), sem("out_stored")
        waits_passed = sem("waits_passed")
        dve_self = sem("dve_self")
        setup_done, zeros_done = sem("setup_done"), sem("zeros_done")
        x_turned, x_evac, stats_done, mean_done, mean_taken, var_done = map(
            sem, ("x_turned", "x_evac", "stats_done", "mean_done", "mean_taken", "var_done"))
        var_ready, scale_ready, row_normed, region_sums = map(sem, ("var_ready", "scale_ready", "row_normed", "region_sums"))
        var_eps, rstd_ready = sem("var_eps"), sem("rstd_ready")
        v_proj, k_proj, v_evac, k_evac, v_turned, v_tok_evac, pad_clear, pad_evac = map(
            sem, ("v_proj", "k_proj", "v_evac", "k_evac", "v_turned", "v_tok_evac", "pad_clear", "pad_evac"))
        means_proj, means_evac, affinity_done, top_done, lepe_done = map(
            sem, ("means_proj", "means_evac", "affinity_done", "top_done", "lepe_done"))
        v_tok_evac_dve = sem("v_tok_evac_dve")
        taps_done, taps_added, lepe_begun = sem("taps_done"), sem("taps_added"), sem("lepe_begun")
        taps_a, taps_last, taps_b = sem("taps_a"), sem("taps_last"), sem("taps_b")
        q_proj, q_evac_act, q_evac_dve = sem("q_proj"), sem("q_evac_act"), sem("q_evac_dve")
        k_sel_done, scores_done, max_done, exp_done, probs_done = map(
            sem, ("k_sel_done", "scores_done", "max_done", "exp_done", "probs_done"))
        probs_turned, probs_t_evac, attn_done, o_row_done, out_proj, out_evac, resid_ready = map(
            sem, ("probs_turned", "probs_t_evac", "attn_done", "o_row_done", "out_proj", "out_evac", "resid_ready"))

        def by_region(flat):
            return flat.rearrange("p (g r c) -> p r g c", g=NWIN, r=RS)

        def by_image(flat):
            return flat.rearrange("p (r g c) -> p r g c", r=RS, g=NWIN)

        def q_block(s, k, h):
            return q_blocks[s, k, :, h, :].rearrange("p g (r c) -> p r g c", r=RS)

        def lepe_row(k, rr):
            return lepe[:, k, bass.ds(rr * ROW, ROW)].rearrange("p (r c) -> p r c", c=W)

        def tap_input(t, k, rr):
            return v_pad[:, k, bass.ds(rr * RS + t // 3, RS), t % 3:t % 3 + W]

        def slot_uses(g, rc):
            return g * SLOT.count(SLOT[rc]) + SLOT[:rc + 1].count(SLOT[rc])

        def before(r, rc):
            return r - BACK[rc] + 1

        N_WEIGHTS = 8

        def chosen(eng, rr, rc):
            word = eng.value_load(idx_row[0:1, bass.ds(rr * NWIN + rc, 1)])
            return [nc.s_assert_within((word >> (IDX_BITS * j)) & (2 ** IDX_BITS - 1), 0, NREG - 1,
                                       skip_runtime_bounds_check_because="max_index gives one of the 49 regions")
                    for j in range(TOPK)]

        def wait_alone(eng, semaphore, value):
            eng.wait_ge(semaphore, value)
            eng.sem_inc(waits_passed, 1)

        block = ctx.enter_context(nc.Block())

        @block.sync
        def _(sp):
            sp.dma_start(x_in, x_img[0]).then_inc(x_in_done, 16)
            sp.dma_start(ident[:], ident_d).then_inc(weights_in, 16)
            sp.dma_start(group[:], group_d).then_inc(weights_in, 16)
            sp.dma_start(wqkv[:], w_qkv.rearrange("(k p) o -> p k o", p=P)).then_inc(weights_in, 16)
            sp.dma_start(bqkv[:], b_qkv).then_inc(weights_in, 16)
            sp.dma_start(taps[:], w_tap).then_inc(weights_in, 16)
            sp.dma_start(btap[:], b_tap).then_inc(weights_in, 16)
            sp.dma_start(wout[:], w_out.rearrange("(k p) o -> p k o", p=P)).then_inc(weights_in, 16)
            sp.dma_start(bout[:], b_out).then_inc(weights_in, 16)

            sp.sem_inc(out_stored, START)

            def store_row(g):
                sp.wait_ge(out_evac, START + 2 * g + 2)
                sp.dma_start(out_rows[g], resid[:]).then_inc(out_stored, 16)

            def regions(b, rr, first, load_x=False):
                g = b * NWIN + rr
                for rc in range(NWIN):
                    r = g * NWIN + rc
                    reg = chosen(sp, rr, rc)
                    wait_alone(sp, attn_done, START + before(r, rc))
                    for j in BY_DMA:
                        half = RT * (j % 2)
                        sp.dma_start(v_sel[half:half + RT, SLOT[rc], j // 2, :],
                                     v_tok[:, bass.ds(reg[j], 1), :]).then_inc(v_sel_in[SLOT[rc]], 16)
                    if rc == 1 and load_x:
                        sp.wait_ge(lepe_done, NWIN * (b + 1))
                        sp.dma_start(x_in, x_img[b + 1]).then_inc(x_in_done, 16)
                    if rc == 2 and not first:
                        store_row(g - 1)
                    if rc == 4:
                        sp.wait_ge(out_stored, START + 16 * g)
                        sp.dma_start(resid[:], x_rows[g]).then_inc(resid_in, 16)

            def image(b, last):
                sp.wait_ge(top_done, b + 1)
                sp.dma_start(idx_row[:], packed_idx[:, 0:1]).then_inc(idx_in, 16)
                wait_alone(sp, idx_in, 16 * (b + 1))
                wait_alone(sp, v_tok_evac, START + 2 * NWIN * (b + 1))
                wait_alone(sp, v_tok_evac_dve, START + 2 * NWIN * (b + 1))
                regions(b, 0, True)
                with sp.Fori(1, NWIN - 1) as rr:
                    regions(b, rr, False)
                regions(b, NWIN - 1, False, not last)
                store_row(b * NWIN + NWIN - 1)

            with sp.Fori(0, NB - 1) as b:
                image(b, False)
            image(NB - 1, True)
            sp.wait_ge(out_stored, START + 16 * NB * NWIN)

        @block.gpsimd
        def _(pool):
            pool.memset(neg_half[:], -0.5).then_inc(zeros_done, 1)
            pool.memset(q_blocks[:, :, :, :, :], 0.0).then_inc(zeros_done, 1)

            def add_bias(g):
                pool.wait_ge(resid_in, 16 * (g + 1))
                pool.tensor_tensor(resid[:], resid[:], bout[:, :].unsqueeze(1).to_broadcast([TT, NT, C]),
                                   ALU.add).then_inc(resid_ready, 1)

            def gather_keys(r, rc, reg):
                pool.wait_ge(scores_done, START + PAIRS * before(r, rc))
                for j in range(TOPK):
                    last = pool.tensor_copy(k_sel[:, SLOT[rc], :, RT * j:RT * (j + 1)],
                                            k_all[:, :, bass.ds(reg[j] * RT, RT)])
                last.then_inc(k_sel_done, 1)

            def gather_values(r, rc, reg):
                pool.wait_ge(attn_done, START + before(r, rc))
                pool.tensor_copy(v_sel[0:RT, SLOT[rc], 1, :],
                                 v_tok[:, bass.ds(reg[BY_POOL], 1), :].rearrange("p n c -> p (n c)")
                                 ).then_inc(v_sel_done, 1)

            def regions(b, rr, is_last):
                g = b * NWIN + rr
                reg = chosen(pool, rr, 0)
                for rc in range(NWIN):
                    if rc + 1 < NWIN:
                        reg_next = chosen(pool, rr, rc + 1)
                        gather_keys(g * NWIN + rc + 1, rc + 1, reg_next)
                    elif not is_last:
                        gather_keys((g + 1) * NWIN, 0, chosen(pool, rr + 1, 0))
                    gather_values(g * NWIN + rc, rc, reg)
                    reg = reg_next
                add_bias(g)

            def multiply_taps(g, rr, is_last=False):
                wait_alone(pool, pad_evac, START + g + (1 if is_last else 2))
                wait_alone(pool, lepe_begun, START + g)
                for t, k in ((2, 0), (2, 1), (1, 1)):
                    last = pool.tensor_tensor(tap_products[t - 1][:, k, :].rearrange("p (r c) -> p r c", c=W),
                                              tap_input(t, k, rr),
                                              taps[:, k, t:t + 1].unsqueeze(2).to_broadcast([P, RS, W]), ALU.mult)
                last.then_inc(taps_added, 1)

            def add_taps(g, rr):
                row = lepe[:, :, bass.ds(rr * ROW, ROW)]
                wait_alone(pool, taps_done, g + 1)
                wait_alone(pool, taps_added, 2 * g + 1)
                pool.tensor_tensor(row, row, tap_products[0], ALU.add).then_inc(taps_added, 1)
                wait_alone(pool, taps_added, 2 * (g + 1))
                pool.tensor_tensor(row, row, tap_products[1], ALU.add).then_inc(lepe_begun, 1)

            pool.sem_inc(lepe_begun, START)
            pool.wait_ge(weights_in, 16 * N_WEIGHTS)
            with pool.Fori(0, NB) as b:
                pool.wait_ge(zeros_done, 2)
                pool.wait_ge(var_eps, b + 1)
                pool.tensor_tensor(rstd[:], var2[:], neg_half[:], ALU.pow).then_inc(rstd_ready, 1)
                wait_alone(pool, x_turned, KC * NWIN * (b + 1))
                pool.memset(v_pad[:, :, 0:PADW:PADW - 1, :], 0.0).then_inc(pad_clear, 1)
                pool.memset(v_pad[:, :, 1:PADW - 1, 0:PADW:PADW - 1], 0.0).then_inc(pad_clear, 1)
                wait_alone(pool, pad_clear, 2 * (b + 1))
                with pool.Fori(0, NWIN - 1) as rr:
                    multiply_taps(b * NWIN + rr, rr)
                    add_taps(b * NWIN + rr, rr)
                multiply_taps(b * NWIN + NWIN - 1, NWIN - 1, True)
                pool.wait_ge(idx_in, 16 * (b + 1))
                wait_alone(pool, k_evac, START + KC * NWIN * (b + 1))
                gather_keys(b * NREG, 0, chosen(pool, 0, 0))
                add_taps(b * NWIN + NWIN - 1, NWIN - 1)
                with pool.Fori(0, NWIN - 1) as rr:
                    regions(b, rr, False)
                regions(b, NWIN - 1, True)

        @block.scalar
        def _(act):
            act.wait_ge(weights_in, 16 * N_WEIGHTS)
            act.wait_ge(setup_done, 1)

            for s in (x_evac, pad_evac, k_evac, v_tok_evac, probs_t_evac):
                act.sem_inc(s, START)

            def normalize(rr):
                for k in range(KC):
                    act.activation(xn[:, k, bass.ds(rr * ROW, ROW)], xn[:, k, bass.ds(rr * ROW, ROW)], ACT.Identity,
                                   bias=shift[:, k:k + 1], scale=rstd[:, k:k + 1]).then_inc(row_normed, 1)

            def multiply_taps(g, rr, is_last=False):
                act.wait_ge(pad_evac, START + g + (1 if is_last else 2))
                act.wait_ge(lepe_begun, START + g)
                for k in range(KC):
                    act.activation(lepe_row(k, rr), tap_input(0, k, rr), ACT.Identity,
                                   bias=btap[:, k:k + 1], scale=taps[:, k, 0:1])
                act.activation(tap_products[0][:, 0, :].rearrange("p (r c) -> p r c", c=W),
                               tap_input(1, 0, rr), ACT.Copy, scale=taps[:, 0, 1:2]).then_inc(taps_done, 1)

            def qkv_row(b, rr, first, last):
                g = b * NWIN + rr
                act.wait_ge(v_turned, START + 4 * g)
                for k in range(KC):
                    act.wait_ge(v_proj, KC * g + k + 1)
                    act.activation(by_region(v_row[:, k, :]), by_image(bank[2 + k][:, 0:ROW]), ACT.Identity,
                                   bias=bqkv[:, 2 * KC + k:2 * KC + k + 1]).then_inc(v_evac, 1)
                    ins = act.activation(v_pad[:, k, bass.ds(rr * RS + 1, RS), 1:1 + W],
                                         bank[2 + k][:, 0:ROW].rearrange("p (r c) -> p r c", c=W), ACT.Identity,
                                         bias=bqkv[:, 2 * KC + k:2 * KC + k + 1])
                ins.then_inc(pad_evac, 1)
                if not last:
                    normalize(rr + 1)
                for k in range(KC):
                    act.wait_ge(k_proj, KC * g + k + 1)
                    act.activation(by_region(k_all[:, k, bass.ds(rr * ROW, ROW)]), by_image(bank[k][:, 0:ROW]),
                                   ACT.Identity, bias=bqkv[:, KC + k:KC + k + 1]).then_inc(k_evac, 1)
                if not first:
                    multiply_taps(g - 1, rr - 1)
                for m in (2, 3):
                    act.wait_ge(v_turned, START + 4 * g + m + 1)
                    n = min(2, NWIN - 2 * m)
                    act.copy(v_tok[:, bass.ds(rr * NWIN + 2 * m, n), :],
                             bank[4 + m][0:RT, 0:n * C].rearrange("p (n c) -> p n c", n=n)).then_inc(v_tok_evac, 1)

            def q_evac(g, k):
                act.wait_ge(q_proj, KC * g + k + 1)
                for h in range(HG // 2):
                    s = slice(HD * h, HD * (h + 1))
                    last = act.activation(q_block(s, k, h), by_image(bank[7][s, 0:ROW]), ACT.Identity,
                                          bias=bq_scaled[s, k:k + 1], scale=SCALE)
                last.then_inc(q_evac_act, 1)

            def probs_t_out(r, k):
                act.wait_ge(probs_turned, KC * r + k + 1)
                if k == 0:
                    act.wait_ge(attn_done, START + r)
                act.copy(probs_t[:, k, :], bank[4 + k][:, :]).then_inc(probs_t_evac, 1)

            def exp(r, p):
                act.wait_ge(max_done, PAIRS * r + p + 1)
                act.activation(probs[:, p, :], bank[p][:, 0:KEYS], ACT.Exp, bias=neg_max[:, p:p + 1],
                               accum_out=denom[:, p:p + 1]).then_inc(exp_done, 1)

            def regions(b, rr, last):
                g = b * NWIN + rr
                for rc in range(NWIN):
                    r = g * NWIN + rc
                    more = not (last and rc == NWIN - 1)
                    if more:
                        exp(r + 1, 0)
                    if rc == NWIN - 1 and not last:
                        q_evac(g + 1, 1)
                    if more:
                        exp(r + 1, 1)
                    probs_t_out(r, 0)
                    if rc == NWIN - 2 and not last:
                        q_evac(g + 1, 0)
                    probs_t_out(r, 1)
                    if more:
                        exp(r + 1, 2)
                        exp(r + 1, 3)

            def x_out(b):
                for n in range(X_TILES):
                    t, k = divmod(n, KC)
                    act.wait_ge(x_turned, X_TILES * b + n + 1)
                    act.copy(xn[:, k, ROW * t:ROW * (t + 1)], bank[n % 4][:, 0:ROW]).then_inc(x_evac, 1)

            def image(b, last):
                act.wait_ge(scale_ready, b + 1)
                wait_alone(act, pad_clear, 2 * (b + 1))
                normalize(0)
                qkv_row(b, 0, True, False)
                with act.Fori(1, NWIN - 1) as rr:
                    qkv_row(b, rr, False, False)
                qkv_row(b, NWIN - 1, False, True)
                act.wait_ge(means_proj, b + 1)
                for m in range(2 * KC):
                    act.activation(qk_mean[:, m, :], bank[0][:, NREG * m:NREG * (m + 1)], ACT.Identity,
                                   bias=bqkv[:, m:m + 1], scale=1.0 / RT).then_inc(means_evac, 1)
                multiply_taps(b * NWIN + NWIN - 1, NWIN - 1, True)
                for k in range(KC):
                    q_evac(b * NWIN, k)
                for p in range(PAIRS):
                    exp(b * NREG, p)
                with act.Fori(0, NWIN - 1) as rr:
                    regions(b, rr, False)
                regions(b, NWIN - 1, True)
                if not last:
                    x_out(b + 1)

            x_out(0)
            with act.Fori(0, NB - 1) as b:
                image(b, False)
            image(NB - 1, True)

        @block.vector
        def _(dve):
            own = [0]

            def settle(ins, base):
                own[0] += 1
                ins.then_inc(dve_self, 1)
                wait_alone(dve, dve_self, base + own[0])

            dve.wait_ge(weights_in, 16 * N_WEIGHTS)
            dve.tensor_scalar(bq_scaled[:], bqkv[:, 0:KC], SCALE, None, ALU.mult).then_inc(setup_done, 1)

            PER_REGION = PAIRS
            SELF_A2 = 2
            SELF_TOP = 5
            IN_B = SELF_A2 + SELF_TOP
            PER_IMAGE = IN_B + NREG * PER_REGION

            COUNT_A = LATE - KC + (NWIN - 2) * IN_A
            COUNT_LAST = IN_A
            COUNT_B = (NWIN - 1) * (LATE - KC - IN_A)

            def add_late_taps(b, rr, steps, counter, before):
                for i in steps:
                    t, k = EARLY_TAPS + i // KC, i % KC
                    if i == 0:
                        dve.wait_ge(lepe_begun, START + b * NWIN + rr + 1)
                    if i >= KC and not (counter is taps_b and i < IN_A + KC):
                        dve.wait_ge(counter, before + i - KC + 1)
                    ins = dve.scalar_tensor_tensor(lepe_row(k, rr), tap_input(t, k, rr), taps[:, k, t:t + 1],
                                                   lepe_row(k, rr), ALU.mult, ALU.add)
                    if i < LATE - KC:
                        ins.then_inc(counter, 1)
                    elif i == LATE - 1:
                        ins.then_inc(lepe_done, 1)

            def late_taps_in_a(b, rr):
                add_late_taps(b, rr, range(IN_A), taps_a, b * COUNT_A + LATE - KC + (rr - 1) * IN_A)

            def late_taps_of_last(b, start, stop):
                add_late_taps(b, NWIN - 1, range(start, stop), taps_last, b * COUNT_LAST)

            def late_taps_in_b(b, rr, start, stop, last_too):
                if start == 0 and stop:
                    dve.wait_ge(taps_a, (b + 1) * COUNT_A)
                    if last_too:
                        dve.wait_ge(taps_last, (b + 1) * COUNT_LAST)
                add_late_taps(b, rr, range(IN_A + start, IN_A + stop), taps_b,
                              b * COUNT_B + (rr - 1) * (LATE - KC - IN_A) - IN_A)

            def v_tok_out(b, rr):
                for m in range(2):
                    dve.wait_ge(v_turned, START + 4 * (b * NWIN + rr) + m + 1)
                    dve.tensor_copy(v_tok[:, bass.ds(rr * NWIN + 2 * m, 2), :],
                                    bank[4 + m][0:RT, :].rearrange("p (n c) -> p n c", n=2)).then_inc(v_tok_evac_dve, 1)

            def sums_row(b, rr):
                dve.wait_ge(row_normed, KC * (b * NWIN + rr + 1))
                for k in range(KC):
                    ins = dve.tensor_reduce(
                        x_sum[:, k, bass.ds(rr * NWIN, NWIN)],
                        xn[:, k, bass.ds(rr * ROW, ROW)].rearrange("p (r g c) -> p g r c", r=RS, g=NWIN), AX.XY, ALU.add)
                ins.then_inc(region_sums, 1)

            for s in (out_evac, o_row_done, v_tok_evac_dve):
                dve.sem_inc(s, START)

            def q_evac(g, k):
                dve.wait_ge(q_proj, KC * g + k + 1)
                for h in range(HG // 2, HG):
                    s = slice(HD * h, HD * (h + 1))
                    last = dve.tensor_scalar(q_block(s, k, h), by_image(bank[7][s, 0:ROW]), SCALE,
                                             bq_scaled[s, k:k + 1], ALU.mult, ALU.add)
                last.then_inc(q_evac_dve, 1)

            def out_half(g, m):
                if m == 0:
                    dve.wait_ge(resid_ready, g + 1)
                dve.wait_ge(out_proj, 2 * g + m + 1)
                dve.tensor_tensor(resid[:, 2 * m:2 * m + 2, :],
                                  bank[7][0:TT, :].rearrange("p (j c) -> p j c", j=2),
                                  resid[:, 2 * m:2 * m + 2, :], ALU.add).then_inc(out_evac, 1)

            def maximum(r, p):
                dve.wait_ge(scores_done, START + PAIRS * r + p + 1)
                dve.tensor_reduce(neg_max[:, p:p + 1], bank[p][:, 0:KEYS], AX.X, ALU.max,
                                  negate=True).then_inc(max_done, 1)

            def invert(r, p):
                dve.wait_ge(exp_done, PAIRS * r + p + 1)
                dve.reciprocal(rdenom[:, p:p + 1], denom[:, p:p + 1]).then_inc(dve_self, 1)

            def divide(p, base):
                dve.wait_ge(dve_self, base + p + 1)
                dve.tensor_scalar(probs[:, p, :], probs[:, p, :], rdenom[:, p:p + 1], None,
                                  ALU.mult).then_inc(probs_done, 1)

            def take_region(r, rr, rc):
                dve.wait_ge(attn_done, START + r + 1)
                cols = slice(RS * rc, RS * (rc + 1))
                dve.tensor_tensor(o_row[:, :, :].rearrange("p k (r c) -> p k r c", c=W)[:, :, :, cols],
                                  bank[6][:, 0:KC * RT].rearrange("p (k r c) -> p k r c", k=KC, r=RS),
                                  lepe[:, :, bass.ds(rr * ROW, ROW)].rearrange("p k (r c) -> p k r c", c=W)[:, :, :, cols],
                                  ALU.add).then_inc(o_row_done, 1)

            def normalized(r, p, base):
                invert(r, p)
                divide(p, base)

            def regions(b, rr, first, last, steps=None, last_steps=None):
                g = b * NWIN + rr

                def beside(rc):
                    if steps:
                        late_taps_in_b(b, rr + 1, sum(steps[:rc]), sum(steps[:rc + 1]), not first and not last_steps)
                    if last_steps:
                        late_taps_of_last(b, sum(last_steps[:rc]), sum(last_steps[:rc + 1]))

                for rc in range(NWIN):
                    r = g * NWIN + rc
                    base = b * PER_IMAGE + IN_B + (rr * NWIN + rc) * PER_REGION
                    more = not (last and rc == NWIN - 1)
                    if more:
                        maximum(r + 1, 0)
                    normalized(r, 2, base)
                    if rc == NWIN - 1 and not first:
                        beside(rc)
                    if rc == NWIN - 1 and not last:
                        q_evac(g + 1, 1)
                    if more:
                        maximum(r + 1, 1)
                    normalized(r, 3, base)
                    if rc == 1 and not first:
                        beside(rc)
                        out_half(g - 1, 1)
                    if more:
                        normalized(r + 1, 0, base + PER_REGION)
                    if rc:
                        take_region(r - 1, rr, rc - 1)
                    elif not first:
                        take_region(r - 1, rr - 1, NWIN - 1)
                    if first or 1 < rc < NWIN - 1:
                        beside(rc)
                    if rc == NWIN - 2 and not last:
                        q_evac(g + 1, 0)
                    if more:
                        maximum(r + 1, 2)
                    if more:
                        normalized(r + 1, 1, base + PER_REGION)
                        maximum(r + 1, 3)
                    if rc == 0 and not first:
                        beside(rc)
                        out_half(g - 1, 0)

            def x_stats(b, tiles):
                for n in tiles:
                    t, k = divmod(n, KC)
                    dve.wait_ge(x_evac, START + X_TILES * b + n + 1)
                    ins = dve.bn_stats(stats[:, k, t, :], xn[:, k, ROW * t:ROW * (t + 1)])
                    if n == X_TILES - 1:
                        ins.then_inc(stats_done, 1)

            def image(b, is_last):
                wait_alone(dve, stats_done, b + 1)
                own[0] = 0
                base = b * PER_IMAGE
                for k in range(KC):
                    last = dve.bn_aggr(mv[:, k, :], stats[:, k, :, :])
                last.then_inc(mean_done, 1)
                dve.wait_ge(mean_taken, b + 1)
                settle(dve.tensor_tensor(dev[:], mv[:, :, 0], bank[4][:, 0:KC], ALU.subtract), base)
                settle(dve.tensor_tensor(dev[:], dev[:], dev[:], ALU.mult), base)
                dve.tensor_tensor(var2[:], dev[:], mv[:, :, 1], ALU.add).then_inc(var_done, 1)
                dve.wait_ge(var_ready, b + 1)
                dve.tensor_scalar(var2[:], bank[5][:, 0:KC], EPS, None, ALU.add).then_inc(var_eps, 1)
                dve.wait_ge(rstd_ready, b + 1)
                dve.scalar_tensor_tensor(shift[:], bank[4][:, 0:KC], -1.0, rstd[:], ALU.mult,
                                         ALU.mult).then_inc(scale_ready, 1)
                sums_row(b, 0)
                sums_row(b, 1)
                v_tok_out(b, 0)
                sums_row(b, 2)
                v_tok_out(b, 1)
                add_late_taps(b, 0, range(LATE), taps_a, b * COUNT_A)
                with dve.Fori(2, NWIN - 1) as rr:
                    sums_row(b, rr + 1)
                    v_tok_out(b, rr)
                    late_taps_in_a(b, rr - 1)
                v_tok_out(b, NWIN - 1)
                own[0] = SELF_A2
                dve.wait_ge(affinity_done, b + 1)
                settle(dve.tensor_copy(affinity[:], bank[6][0:NREG, 0:NREG]), base)
                settle(dve.max(top[:], affinity[:]), base)
                settle(dve.max_index(top_idx[:], top[:], affinity[:]), base)
                word = top_idx[:, TOPK - 1:TOPK]
                for j in range(TOPK - 2, -1, -1):
                    ins = dve.scalar_tensor_tensor(packed_idx[:, j:j + 1], word, float(2 ** IDX_BITS),
                                                   top_idx[:, j:j + 1], ALU.mult, ALU.add)
                    word = packed_idx[:, j:j + 1]
                    if j:
                        settle(ins, base)
                    else:
                        ins.then_inc(top_done, 1)
                q_evac(b * NWIN, 0)
                late_taps_in_a(b, NWIN - 2)
                q_evac(b * NWIN, 1)
                for p in range(PAIRS):
                    maximum(b * NREG, p)
                for p in range(2):
                    normalized(b * NREG, p, base + IN_B)
                regions(b, 0, True, False, STEPS_ROW_0)
                regions(b, 1, False, False, STEPS, STEPS_OF_LAST)
                with dve.Fori(2, NWIN - 1) as rr:
                    regions(b, rr, False, False, STEPS)
                regions(b, NWIN - 1, False, True)
                if not is_last:
                    x_stats(b + 1, range(X_AHEAD))
                take_region(b * NREG + NREG - 1, NWIN - 1, NWIN - 1)
                if not is_last:
                    x_stats(b + 1, range(X_AHEAD, X_TILES))
                for m in range(2):
                    out_half(b * NWIN + NWIN - 1, m)

            x_stats(0, range(X_TILES))
            with dve.Fori(0, NB - 1) as b:
                image(b, False)
            image(NB - 1, True)

        @block.tensor
        def _(pe):
            pe.wait_ge(weights_in, 16 * N_WEIGHTS)
            pe.wait_ge(zeros_done, 2)

            def project(dst, col, rr, done):
                for k in range(KC):
                    last = pe.matmul(dst[:, 0:ROW], wqkv[:, k, col:col + P], xn[:, k, bass.ds(rr * ROW, ROW)],
                                     start=(k == 0), stop=(k == KC - 1))
                last.then_inc(done, 1)

            for s in (scores_done, attn_done, v_turned):
                pe.sem_inc(s, START)

            def project_q(g, rr, k):
                if k:
                    pe.wait_ge(q_evac_act, KC * g + 1)
                    pe.wait_ge(q_evac_dve, KC * g + 1)
                else:
                    pe.wait_ge(out_evac, START + 2 * (g - 1))
                project(bank[7], P * k, rr, q_proj)

            def out_half(g, m):
                if m == 0:
                    pe.wait_ge(o_row_done, START + NWIN * (g + 1))
                pe.wait_ge(out_evac, START + 2 * g + m)
                for j in (2 * m, 2 * m + 1):
                    for k in range(KC):
                        last = pe.matmul(bank[7][0:TT, C * (j % 2):C * (j % 2 + 1)],
                                         o_row[:, k, TT * j:TT * (j + 1)], wout[:, k, :],
                                         start=(k == 0), stop=(k == KC - 1))
                last.then_inc(out_proj, 1)

            def scores(r, g, rc, p):
                k, h = divmod(2 * p, HG)
                if p == 0:
                    pe.wait_ge(k_sel_done, r + 1)
                if rc == 0 and h == 0:
                    pe.wait_ge(q_evac_act, KC * g + k + 1)
                    pe.wait_ge(q_evac_dve, KC * g + k + 1)
                pe.matmul(bank[p][:, 0:KEYS], q_blocks[:, k, rc, h:h + 2, :].rearrange("p h t -> p (h t)"),
                          k_sel[:, SLOT[rc], k, :], start=True, stop=True).then_inc(scores_done, 1)

            def turn_probs(r, p):
                k = p // 2
                if p % 2 == 0:
                    pe.wait_ge(probs_t_evac, START + KC * (r - 1) + k + 1)
                pe.wait_ge(probs_done, PAIRS * r + p + 1)
                for c in range(CH):
                    at = P * (CH * (p % 2) + c)
                    t = pe.transpose(bank[4 + k][:, at:at + P], probs[:, p, P * c:P * (c + 1)], ident[:])
                if p % 2:
                    t.then_inc(probs_turned, 1)

            def attend(g, r, rc):
                pe.wait_ge(v_sel_in[SLOT[rc]], 16 * len(BY_DMA) * slot_uses(g, rc))
                pe.wait_ge(v_sel_done, r + 1)
                pe.wait_ge(o_row_done, START + r)
                for k in range(KC):
                    pe.wait_ge(probs_t_evac, START + KC * r + k + 1)
                    for c in range(CH):
                        for h in range(HG):
                            head = HG * k + h
                            at = RT * (2 * CH * (h // 2) + 2 * c + h % 2)
                            last = pe.matmul(bank[6][HD * h:HD * (h + 1), RT * k:RT * (k + 1)],
                                             v_sel[:, SLOT[rc], c, HD * head:HD * (head + 1)],
                                             probs_t[:, k, at:at + RT],
                                             start=(c == 0), stop=(c == CH - 1))
                last.then_inc(attn_done, 1)

            def regions(b, rr, first, last):
                g = b * NWIN + rr
                for rc in range(NWIN):
                    r = g * NWIN + rc
                    for p in range(PAIRS):
                        turn_probs(r, p)
                        if rc + 1 < NWIN:
                            scores(r + 1, g, rc + 1, p)
                        elif not last:
                            scores(r + 1, g + 1, 0, p)
                        if p == 1 and rc == 1 and not first:
                            out_half(g - 1, 1)
                        if p == 0 and rc == NWIN - 1 and not last:
                            project_q(g + 1, rr + 1, 1)
                        if p == 1 and rc:
                            attend(g, r - 1, rc - 1)
                        elif p == 1 and not first:
                            attend(g - 1, r - 1, NWIN - 1)
                        if p == 1 and rc == NWIN - 2 and not last:
                            project_q(g + 1, rr + 1, 0)
                        if p == PAIRS - 1 and rc == 0 and not first:
                            out_half(g - 1, 0)

            def turn_x(b, tiles):
                for n in tiles:
                    t, k = divmod(n, KC)
                    if n == 0:
                        pe.wait_ge(x_in_done, 16 * (b + 1))
                    if n >= 4:
                        pe.wait_ge(x_evac, START + X_TILES * b + n - 3)
                    for j in range(NT):
                        last = pe.transpose(bank[n % 4][:, TT * j:TT * (j + 1)],
                                            x_in[:, NT * t + j, P * k:P * (k + 1)], ident[0:TT, 0:TT])
                    last.then_inc(x_turned, 1)

            def image(b, is_last):
                pe.wait_ge(mean_done, b + 1)
                pe.matmul(bank[4][:, 0:KC], group[:], mv[:, :, 0], start=True, stop=True).then_inc(mean_taken, 1)
                pe.wait_ge(var_done, b + 1)
                pe.matmul(bank[5][:, 0:KC], group[:], var2[:], start=True, stop=True).then_inc(var_ready, 1)
                pe.wait_ge(scale_ready, b + 1)
                wait_alone(pe, x_evac, START + KC * NWIN * (b + 1))
                with pe.Fori(0, NWIN) as rr:
                    g = b * NWIN + rr
                    pe.wait_ge(row_normed, KC * (g + 1))
                    pe.wait_ge(pad_evac, START + g)
                    for k in range(KC):
                        project(bank[2 + k], 2 * C + P * k, rr, v_proj)
                    pe.wait_ge(k_evac, START + KC * g)
                    for k in range(KC):
                        project(bank[k], C + P * k, rr, k_proj)
                    pe.wait_ge(v_evac, KC * (g + 1))
                    wait_alone(pe, v_tok_evac, START + 2 * g)
                    wait_alone(pe, v_tok_evac_dve, START + 2 * g)
                    for reg in range(NWIN):
                        for k in range(KC):
                            at = C * (reg % 2) + P * k
                            last = pe.transpose(bank[4 + reg // 2][0:RT, at:at + P],
                                                v_row[:, k, RT * reg:RT * (reg + 1)], ident[:])
                        if reg % 2 or reg == NWIN - 1:
                            last.then_inc(v_turned, 1)
                pe.wait_ge(region_sums, NWIN * (b + 1))
                pe.wait_ge(k_evac, START + KC * NWIN * (b + 1))
                for m in range(2 * KC):
                    for k in range(KC):
                        last = pe.matmul(bank[0][:, NREG * m:NREG * (m + 1)], wqkv[:, k, P * m:P * (m + 1)],
                                         x_sum[:, k, :], start=(k == 0), stop=(k == KC - 1))
                last.then_inc(means_proj, 1)
                pe.wait_ge(v_tok_evac, START + 2 * NWIN * (b + 1))
                project_q(b * NWIN, 0, 0)
                pe.wait_ge(means_evac, 2 * KC * (b + 1))
                for k in range(KC):
                    last = pe.matmul(bank[6][0:NREG, 0:NREG], qk_mean[:, k, :], qk_mean[:, KC + k, :],
                                     start=(k == 0), stop=(k == KC - 1))
                last.then_inc(affinity_done, 1)
                project_q(b * NWIN, 0, 1)
                for p in range(PAIRS):
                    scores(b * NREG, b * NWIN, 0, p)
                regions(b, 0, True, False)
                with pe.Fori(1, NWIN - 1) as rr:
                    regions(b, rr, False, False)
                regions(b, NWIN - 1, False, True)
                if not is_last:
                    turn_x(b + 1, range(X_AHEAD))
                attend(b * NWIN + NWIN - 1, b * NREG + NREG - 1, NWIN - 1)
                if not is_last:
                    turn_x(b + 1, range(X_AHEAD, X_TILES))
                for m in range(2):
                    out_half(b * NWIN + NWIN - 1, m)

            turn_x(0, range(X_TILES))
            with pe.Fori(0, NB - 1) as b:
                image(b, False)
            image(NB - 1, True)


def kernel(x, L0_conv_qkv_w, L0_conv_qkv_b, L0_conv_lepe_w, L0_conv_lepe_b, L0_conv_out_w, L0_conv_out_b):
    import numpy as np
    import concourse.bacc as bacc
    from concourse.bass_utils import run_bass_kernel_spmd as run

    def chunked(a):
        a = np.asarray(a)
        return np.ascontiguousarray(np.moveaxis(a.reshape(-1, P, *a.shape[1:]), 0, 1))

    arrays = {
        "x": np.ascontiguousarray(np.asarray(x).reshape(NB * NWIN, ROW, C)),
        "w_qkv": np.ascontiguousarray(np.asarray(L0_conv_qkv_w).T),
        "w_out": np.ascontiguousarray(np.asarray(L0_conv_out_w).T),
        "b_qkv": chunked(L0_conv_qkv_b),
        "b_out": np.ascontiguousarray(np.broadcast_to(np.asarray(L0_conv_out_b), (TT, C))),
        "w_tap": chunked(np.asarray(L0_conv_lepe_w).reshape(C, TAPS)),
        "b_tap": chunked(L0_conv_lepe_b),
        "ident": np.eye(P, dtype=np.float32),
        "group": np.kron(np.eye(P // GROUP), np.full((GROUP, GROUP), 1.0 / GROUP)).astype(np.float32),
    }
    nc = bacc.Bacc("TRN2", target_bir_lowering=False, num_devices=1)
    args = [nc.dram_tensor(f"{n}_dram", list(a.shape), F32, kind="ExternalInput").ap() for n, a in arrays.items()]
    out = nc.dram_tensor("out_dram", [NB * NWIN, ROW, C], F32, kind="ExternalOutput").ap()
    attention_kernel(nc, *args, out)
    r = run(nc, [{f"{n}_dram": a for n, a in arrays.items()}], core_ids=[0])
    return r.results[0]["out_dram"].reshape(NB, H, W, C)
```
